# Optimizing a Trainium2 kernel written in Bass

```python
import numpy as np
import jax
import jax.numpy as jnp

def _softmax(x, axis=-1):
    return jax.nn.softmax(x, axis=axis)

def _gelu(x):
    return jax.nn.gelu(x, approximate=True)

def _silu(x):
    return jax.nn.silu(x)

def _sigmoid(x):
    return jax.nn.sigmoid(x)

def _layernorm(x, axis=-1, eps=1e-05):
    m = jnp.mean(x, axis=axis, keepdims=True)
    v = jnp.var(x, axis=axis, keepdims=True)
    return (x - m) / jnp.sqrt(v + eps)

def _scatter_add(tgt, idx, src, axis=0):
    return tgt.at[idx].add(src)

def _segment_sum(src, seg, n):
    return jax.ops.segment_sum(src, seg, n)
kernel_name = 'mk_gnn_ffn_d1_gnn_r8_e90bd3'

def setup_inputs(seed: int=0):
    np.random.seed(seed)
    _w = jnp.asarray

    def _rec_inputs():
        import jax
        import jax.numpy as jnp
        _gk = jax.random.key(seed)
        x = -8.776e-05 + 1 * jax.random.normal(jax.random.fold_in(_gk, 1), (1250, 512), jnp.float32)
        src = jax.random.randint(jax.random.fold_in(_gk, 2), (20000,), 0, 1250, jnp.int32)
        dst = jax.random.randint(jax.random.fold_in(_gk, 3), (20000,), 0, 1250, jnp.int32)
        _o = jnp.argsort(dst, stable=True)
        src = src[_o]
        dst = dst[_o]
        return (x, src, dst)
    x, src, dst = _rec_inputs()

    def _L0_gnn_setup():
        import jax, jax.numpy as jnp
        import numpy as np
        N_NODES = 1250
        N_EDGES = 20000
        DIM = 512
        LN_EPS = 1e-05
        key = jax.random.key(seed)
        ks = jax.random.split(key, 6)
        scale = 1.0 / np.sqrt(DIM)
        h = jax.random.normal(ks[0], (N_NODES, DIM), dtype=jnp.float32)
        edge_index = jax.random.randint(ks[1], (2, N_EDGES), 0, N_NODES, dtype=jnp.int32)
        W_self = jax.random.normal(ks[2], (DIM, DIM), dtype=jnp.float32) * scale
        b_self = jnp.zeros((DIM,), dtype=jnp.float32)
        W_neigh = jax.random.normal(ks[3], (DIM, DIM), dtype=jnp.float32) * scale
        b_neigh = jnp.zeros((DIM,), dtype=jnp.float32)
        ln_gamma = jnp.ones((DIM,), dtype=jnp.float32)
        ln_beta = jnp.zeros((DIM,), dtype=jnp.float32)
        return {'h': h, 'edge_index': edge_index, 'W_self': W_self, 'b_self': b_self, 'W_neigh': W_neigh, 'b_neigh': b_neigh, 'ln_gamma': ln_gamma, 'ln_beta': ln_beta}
    _L0_gnn_all = _L0_gnn_setup()
    _L0_gnn_in = {k: v for k, v in _L0_gnn_all.items() if k in ('W_self', 'b_self', 'W_neigh', 'b_neigh', 'ln_gamma', 'ln_beta')}
    del _L0_gnn_all

    def _L0_ffn_setup():
        import jax, jax.numpy as jnp
        import numpy as np
        E = 64
        K = 2
        CAP = 512
        H = 512
        FFN = 256
        B, S = (8, 512)
        key = jax.random.key(seed)
        ks = jax.random.split(key, 6)
        hidden_states = jax.random.normal(ks[0], (B, S, H), dtype=jnp.float32)
        router_w = jax.random.normal(ks[1], (E, H), dtype=jnp.float32) * (0.01 / np.sqrt(H))
        w1 = jax.random.normal(ks[2], (FFN, H), dtype=jnp.float32) * (1.0 / np.sqrt(H))
        b1 = jnp.zeros((FFN,), dtype=jnp.float32)
        w2 = jax.random.normal(ks[3], (H, FFN), dtype=jnp.float32) * (1.0 / np.sqrt(FFN))
        b2 = jnp.zeros((H,), dtype=jnp.float32)
        return {'hidden_states': hidden_states, 'router_w': router_w, 'w1': w1, 'b1': b1, 'w2': w2, 'b2': b2}
    _L0_ffn_all = _L0_ffn_setup()
    _L0_ffn_in = {k: v for k, v in _L0_ffn_all.items() if k in ('router_w', 'w1', 'b1', 'w2', 'b2')}
    del _L0_ffn_all
    return {'x': x, 'src': src, 'dst': dst, 'L0_gnn_W_self': _L0_gnn_in['W_self'], 'L0_gnn_b_self': _L0_gnn_in['b_self'], 'L0_gnn_W_neigh': _L0_gnn_in['W_neigh'], 'L0_gnn_b_neigh': _L0_gnn_in['b_neigh'], 'L0_gnn_ln_gamma': _L0_gnn_in['ln_gamma'], 'L0_gnn_ln_beta': _L0_gnn_in['ln_beta'], 'L0_ffn_router_w': _L0_ffn_in['router_w'], 'L0_ffn_w1': _L0_ffn_in['w1'], 'L0_ffn_b1': _L0_ffn_in['b1'], 'L0_ffn_w2': _L0_ffn_in['w2'], 'L0_ffn_b2': _L0_ffn_in['b2']}

def reference(x, src, dst, L0_gnn_W_self, L0_gnn_b_self, L0_gnn_W_neigh, L0_gnn_b_neigh, L0_gnn_ln_gamma, L0_gnn_ln_beta, L0_ffn_router_w, L0_ffn_w1, L0_ffn_b1, L0_ffn_w2, L0_ffn_b2):
    import jax
    import jax.numpy as jnp

    def _L0_gnn_ref(h, edge_index, W_self, b_self, W_neigh, b_neigh, ln_gamma, ln_beta):
        import jax, jax.numpy as jnp
        import numpy as np
        N_NODES = 1250
        N_EDGES = 20000
        DIM = 512
        LN_EPS = 1e-05
        n = h.shape[0]
        src = edge_index[0]
        dst = edge_index[1]
        msg = h[dst] @ W_neigh.T + b_neigh
        neigh = jax.ops.segment_sum(msg, src, num_segments=n)
        deg = jax.ops.segment_sum(jnp.ones(src.shape, h.dtype), src, num_segments=n)
        deg = jnp.maximum(deg, 1.0)
        neigh = neigh / deg[:, None]
        out = jax.nn.relu(h @ W_self.T + b_self + neigh)
        x = h + out
        mean = jnp.mean(x, axis=-1, keepdims=True)
        var = jnp.mean(jnp.square(x - mean), axis=-1, keepdims=True)
        return (x - mean) * jax.lax.rsqrt(var + LN_EPS) * ln_gamma + ln_beta

    def _L0_ffn_ref(hidden_states, router_w, w1, b1, w2, b2):
        import jax, jax.numpy as jnp
        import numpy as np
        E = 64
        K = 2
        CAP = 512
        H = 512
        FFN = 256
        B, S = (8, 512)
        orig_shape = hidden_states.shape
        x = hidden_states.reshape(-1, orig_shape[-1])
        T = x.shape[0]
        N = T * K
        logits = jnp.einsum('th,eh->te', x, router_w)
        probs_full = jax.nn.softmax(logits, axis=-1)
        probs, idx = jax.lax.top_k(probs_full, K)
        flat_e = idx.reshape(-1)
        flat_p = probs.reshape(-1)
        order = jnp.argsort(flat_e, stable=True)
        sorted_e = flat_e[order]
        counts = jnp.zeros((E,), jnp.int32).at[flat_e].add(1)
        offsets = jnp.concatenate([jnp.zeros((1,), jnp.int32), jnp.cumsum(counts)[:-1]])
        pos = jnp.arange(N, dtype=jnp.int32) - offsets[sorted_e]
        keep = pos < CAP
        slot = sorted_e * CAP + jnp.minimum(pos, CAP - 1)
        dest = jnp.where(keep, slot, E * CAP)
        tok = order // K
        buf = jnp.zeros((E * CAP + 1, x.shape[-1]), x.dtype).at[dest].set(x[tok])
        buf = buf[:-1]
        h = jax.nn.gelu(jnp.einsum('nh,fh->nf', buf, w1) + b1, approximate=False)
        y = jnp.einsum('nf,hf->nh', h, w2) + b2
        gate = jnp.where(keep, flat_p[order], 0.0)
        contrib = y[jnp.minimum(slot, E * CAP - 1)] * gate[:, None]
        out = jnp.zeros_like(x).at[tok].add(contrib)
        return out.reshape(orig_shape)
    edge_index = jnp.stack([src, dst])
    x = x + _L0_gnn_ref(_layernorm(x, axis=-1), edge_index, L0_gnn_W_self, L0_gnn_b_self, L0_gnn_W_neigh, L0_gnn_b_neigh, L0_gnn_ln_gamma, L0_gnn_ln_beta)
    x = x + _L0_ffn_ref(_layernorm(x, axis=-1)[None], L0_ffn_router_w, L0_ffn_w1, L0_ffn_b1, L0_ffn_w2, L0_ffn_b2)[0]
    return x

_drawn_inputs = setup_inputs


def setup_inputs(seed=0):
    import zlib

    import numpy as np

    out = dict(_drawn_inputs(seed))
    spreads = {'L0_gnn_b_self': (0.0, 0.1),
     'L0_gnn_b_neigh': (0.0, 0.1),
     'L0_gnn_ln_gamma': (1.0, 0.2),
     'L0_gnn_ln_beta': (0.0, 0.1),
     'L0_ffn_b1': (0.0, 0.8),
     'L0_ffn_b2': (0.0, 2.0)}
    factors = {'L0_ffn_router_w': 8.0, 'L0_ffn_w1': 5.804, 'L0_ffn_w2': 5.23}
    for name, (base, spread) in spreads.items():
        noise = np.random.default_rng([zlib.crc32(name.encode()), seed]).standard_normal(out[name].shape)
        drawn = base * np.exp(spread * noise) if base else spread * noise
        out[name] = jnp.asarray(drawn.astype(out[name].dtype))
    for name, factor in factors.items():
        out[name] = (out[name] * factor).astype(out[name].dtype)
    return out
```

```python
import numpy as np
import concourse.bass as bass
from concourse import mybir
from contextlib import ExitStack

N_NODES, N_EDGES, DIM, FFN, EXPERTS, CAPACITY = 1250, 20000, 512, 256, 64, 512
LN_EPS = 1e-5
ROWS = 125
TILES = N_NODES // ROWS
PAIRS = TILES // 2
KC = DIM // 128
FC = FFN // 128
GROUP = 25
GROUPS = N_NODES // GROUP
PER_TILE = ROWS // GROUP
FIFTHS = 5
FIFTH = N_NODES // FIFTHS
ALIGN = 16
WINDOW = 512
WCHUNKS = WINDOW // 128
STARTS = N_EDGES // ALIGN - WINDOW // ALIGN + 1
SAMPLES = N_EDGES // ALIGN // ROWS
ECHUNKS = N_EDGES // ROWS
SRC_PARTS = [(0, 500), (500, 500), (1000, 250)]
SH, SW, SG, SF = 64.0, 256.0, 64.0, 16.0


def gnn_ffn(nc, x, windows, src, dst, w_neigh_t, w_self_t, b_neigh, b_self, gamma, beta,
            router_t, w1_t, b1, w2_t, b2, out):
    f32, f16, i32, u32 = mybir.dt.float32, mybir.dt.float16, mybir.dt.int32, mybir.dt.uint32
    ALU, ACT, AX = mybir.AluOpType, mybir.ActivationFunctionType, mybir.AxisListType

    with ExitStack() as ctx:
        def sb(name, shape, dt=f32):
            return ctx.enter_context(nc.sbuf_tensor(name, shape, dt))

        def bank(name):
            return ctx.enter_context(nc.psum_tensor(name, [128, 512], f32))

        def sem(name):
            return ctx.enter_context(nc.semaphore(name))

        x_all = sb("x_all", [ROWS, TILES, DIM])
        h_all = sb("h_all", [ROWS, TILES, DIM])
        s_all = sb("s_all", [ROWS, TILES, DIM])
        g_hi = sb("g_hi", [ROWS, TILES, DIM], f16)
        g_lo = sb("g_lo", [ROWS, TILES, DIM], f16)
        adj_flat = sb("adj", [ROWS, TILES * N_NODES], f16)
        adj = adj_flat[:, :].rearrange("p (t n) -> p t n", t=TILES)
        wn_raw = sb("wn_raw", [128, KC, DIM])
        ws_raw = sb("ws_raw", [128, KC, DIM])
        w1_raw = sb("w1_raw", [128, KC, FFN])
        wr_raw = sb("wr_raw", [128, KC, EXPERTS])
        w2_raw = sb("w2_raw", [128, FC, DIM])
        wn_hi, wn_lo = sb("wn_hi", [128, KC, DIM], f16), sb("wn_lo", [128, KC, DIM], f16)
        ws_hi, ws_lo = sb("ws_hi", [128, KC, DIM], f16), sb("ws_lo", [128, KC, DIM], f16)
        w1_hi, w1_lo = sb("w1_hi", [128, KC, FFN], f16), sb("w1_lo", [128, KC, FFN], f16)
        wr_hi, wr_lo = sb("wr_hi", [128, KC, EXPERTS], f16), sb("wr_lo", [128, KC, EXPERTS], f16)
        w2_hi, w2_lo = sb("w2_hi", [128, FC, DIM], f16), sb("w2_lo", [128, FC, DIM], f16)
        bneigh = sb("bneigh", [ROWS, DIM])
        bself = sb("bself", [ROWS, DIM])
        gam = sb("gam", [ROWS, DIM])
        bet = sb("bet", [ROWS, DIM])
        b2_bc = sb("b2_bc", [ROWS, DIM])
        b1_col = sb("b1_col", [128, FC])
        ident = sb("ident", [128, 128])
        iota = sb("iota", [128, N_NODES + 1], f16)
        earlier = sb("earlier", [ROWS, ROWS], f16)
        ones = sb("ones", [ROWS, ROWS], f16)
        onesf = sb("onesf", [128, 1])
        minus_half = sb("minus_half", [ROWS, 2])
        dst_all = sb("dst_all", [ROWS, N_EDGES // ROWS], i32)
        src_all = sb("src_all", [ROWS, N_EDGES // ROWS], i32)
        samples = sb("samples", [ROWS, SAMPLES])
        bounds = sb("bounds", [ROWS, GROUPS])
        below_sum = sb("below_sum", [ROWS, GROUPS])
        start_f = sb("start_f", [GROUPS, 1])
        start_u = sb("start_u", [GROUPS, 1], u32)
        base_col = sb("base_col", [GROUPS, 1])
        n_valid = sb("n_valid", [GROUPS, 1])
        missed = sb("missed", [1, 1], i32)
        key_col = sb("key_col", [128, 2, WCHUNKS, GROUPS])
        hot_row_flat = sb("hot_row", [128, PER_TILE * WCHUNKS * ROWS], f16)
        hot_col_flat = sb("hot_col", [128, PER_TILE * WCHUNKS * FIFTH], f16)
        hot_row = hot_row_flat[:, :].rearrange("p (q c r) -> p q c r", q=PER_TILE, c=WCHUNKS)
        hot_col = hot_col_flat[:, :].rearrange("p (q c r) -> p q c r", q=PER_TILE, c=WCHUNKS)
        count_stage = sb("count_stage", [ROWS, PER_TILE, FIFTH], f16)
        stats = sb("stats", [ROWS, 2, 6])
        mv = sb("mv", [ROWS, 2, 2])
        rstd = sb("rstd", [ROWS, 2, 1])
        ve = sb("ve", [ROWS, 2, 1])
        hT_hi, hT_lo = sb("hT_hi", [128, 2, KC, ROWS], f16), sb("hT_lo", [128, 2, KC, ROWS], f16)
        g_f = sb("g_f", [ROWS, 2, DIM])
        stats1, mv1 = sb("stats1", [ROWS, 2, 6]), sb("mv1", [ROWS, 2, 2])
        stats2, mv2 = sb("stats2", [ROWS, 2, 6]), sb("mv2", [ROWS, 2, 2])
        ve1, rstd1 = sb("ve1", [ROWS, 2, 1]), sb("rstd1", [ROWS, 2, 1])
        ve2, rstd2 = sb("ve2", [ROWS, 2, 1]), sb("rstd2", [ROWS, 2, 1])
        deg = sb("deg", [ROWS, 2, 1])
        inv_deg = sb("inv_deg", [ROWS, 2, 1])
        relu_in = wn_raw[0:ROWS, 0:2, :]
        x1 = wn_raw[0:ROWS, 2:4, :]
        n1 = ws_raw[0:ROWS, 0:2, :]
        n1g = ws_raw[0:ROWS, 2:4, :]
        xn = g_f[:, :, :]
        xT_hi, xT_lo = sb("xT_hi", [128, KC, 2, ROWS], f16), sb("xT_lo", [128, KC, 2, ROWS], f16)
        scratch = adj_flat[0:GROUPS, :]

        def edge_words(first, rows, dt):
            part = scratch[:, 2 * WINDOW * first:2 * WINDOW * (first + rows)].bitcast(dt)
            return part.rearrange("p (a b) -> p a b", a=rows) if rows > 1 else part

        win_i = edge_words(0, 2, i32).rearrange("p a b -> p (a b)")
        win = edge_words(2, 2, f32)
        keys = edge_words(4, 2, f32)
        below = adj_flat[:, 18 * WINDOW:18 * WINDOW + 2 * GROUPS * SAMPLES].bitcast(f32).rearrange(
            "p (g s) -> p g s", g=GROUPS)
        local, valid, fifth = edge_words(6, 1, f32), edge_words(7, 1, f32), edge_words(8, 1, f32)
        wn_room = wn_raw[:, :, :].rearrange("p k n -> p (k n)")
        ws_room = ws_raw[:, :, :].rearrange("p k n -> p (k n)")
        all_counts = wn_room[0:ROWS, 0:N_NODES]
        all_src_hot = wn_room[0:ROWS, N_NODES:N_NODES + N_NODES // 2].bitcast(f16)
        all_dst_hot = wn_room[0:ROWS, 1880:1944].bitcast(f16)[:, 0:ROWS]
        rest = ws_room[0:ROWS, 0:N_NODES // 2].bitcast(f16)
        all_src = ws_room[0:ROWS, 640:640 + ECHUNKS]
        all_dst = ws_room[0:ROWS, 800:800 + ECHUNKS]
        all_deg = ws_room[0:ROWS, 960:960 + TILES]
        all_inv_deg = ws_room[0:ROWS, 976:976 + TILES]
        hot_words = hot_row_flat[:, :]
        hid = hot_words[:, 0:4 * FC * ROWS].bitcast(f32).rearrange("p (f n) -> p f n", f=FC)
        hid_hi = hot_words[:, 4 * FC * ROWS:6 * FC * ROWS].rearrange("p (f n) -> p f n", f=FC)
        hid_lo = hot_words[:, 6 * FC * ROWS:8 * FC * ROWS].rearrange("p (f n) -> p f n", f=FC)
        logits = sb("logits", [ROWS, 2, EXPERTS])
        top = sb("top", [ROWS, 2])
        shifted = sb("shifted", [ROWS, 2, EXPERTS])
        expd = sb("expd", [ROWS, 2, EXPERTS])
        esum = sb("esum", [ROWS, 2])
        rsum = sb("rsum", [ROWS, 2])
        probs = sb("probs", [ROWS, 2, EXPERTS])
        best = sb("best", [ROWS, 2, 8])
        best_at = sb("best_at", [ROWS, 2, 8], u32)
        best_f = sb("best_f", [ROWS, 2, 8])
        first_hot = sb("first_hot", [ROWS, 2, EXPERTS], f16)
        chosen = sb("chosen", [ROWS, 2, EXPERTS], f16)
        chosen_sum = sb("chosen_sum", [ROWS, EXPERTS], f16)
        chosen_p = sb("chosen_p", [ROWS, 2, EXPERTS])
        kept_p = sb("kept_p", [ROWS, 2, EXPERTS])
        gate = sb("gate", [ROWS, 2, 1])
        gate_s = sb("gate_s", [ROWS, 2, 1])
        hot_words = hot_col_flat[0:ROWS, :]
        b2g = hot_words[:, 0:4 * DIM].bitcast(f32).rearrange("p (u n) -> p u n", u=2)
        x2b = hot_words[:, 4 * DIM:8 * DIM].bitcast(f32).rearrange("p (u n) -> p u n", u=2)

        p_T, p_G, p_S, p_A0, p_A1, p_R, p_D, p_P = [bank(n) for n in
            ("p_T", "p_G", "p_S", "p_A0", "p_A1", "p_R", "p_D", "p_P")]
        p_A = [p_A0, p_A1]
        p_N = [p_G, p_S]
        p_H, p_Y = p_A0, p_A1

        src_in = sem("src_in")
        dst_in, win_in, bias_in, w1_in, wr_in, w2_in, wn_in, ws_in = [sem(n) for n in
            ("dst_in", "win_in", "bias_in", "w1_in", "wr_in", "w2_in", "wn_in", "ws_in")]
        x_in = [sem(f"x_in{t}") for t in range(TILES)]
        const_step, const_done = sem("const_step"), sem("const_done")
        below_done, start_counted, start_done = sem("below_done"), sem("start_counted"), sem("start_done")
        keys_done, keys_turned, key_cols_done = sem("keys_done"), sem("keys_turned"), sem("key_cols_done")
        missed_counted, missed_done = sem("missed_counted"), sem("missed_done")
        w_hi_done, w_lo_done = sem("w_hi_done"), sem("w_lo_done")
        dve_step, pool_step = sem("dve_step"), sem("pool_step")
        var_done, rstd_done, h_done, xb_done = sem("var_done"), sem("rstd_done"), sem("h_done"), sem("xb_done")
        hT_made, hT_hi_done, hT_lo_done = sem("hT_made"), sem("hT_hi_done"), sem("hT_lo_done")
        g_made, g_f_done, g_hi_done, g_lo_done = sem("g_made"), sem("g_f_done"), sem("g_hi_done"), sem("g_lo_done")
        s_made, s_raw_done, s_done = sem("s_made"), sem("s_raw_done"), sem("s_done")
        hot_done, counts_made, counts_staged = sem("hot_done"), sem("counts_made"), sem("counts_staged")
        counts_moved = [sem(f"counts_moved{q}") for q in range(PER_TILE)]
        neigh_made, deg_read, neigh_read = sem("neigh_made"), sem("deg_read"), sem("neigh_read")
        var1_done, rstd1_done, n1_done, x2_done = sem("var1_done"), sem("rstd1_done"), sem("n1_done"), sem("x2_done")
        var2_done, rstd2_done, xn_done = sem("var2_done"), sem("rstd2_done"), sem("xn_done")
        xT_made, xT_hi_done, xT_lo_done = sem("xT_made"), sem("xT_hi_done"), sem("xT_lo_done")
        logits_made, logits_read, shifted_done, exp_done = (sem("logits_made"), sem("logits_read"),
                                                           sem("shifted_done"), sem("exp_done"))
        chosen_done, sum_done, pos_made, gate_done = sem("chosen_done"), sem("sum_done"), sem("pos_made"), sem("gate_done")
        hid_made, gelu_done, hid_done = sem("hid_made"), sem("gelu_done"), sem("hid_done")
        y_made, x2b_done, out_done, stored = sem("y_made"), sem("x2b_done"), sem("out_done"), sem("stored")

        gen_ready, gen_src_hot, gen_deg_made, gen_deg_added = (sem("gen_ready"), sem("gen_src_hot"),
                                                               sem("gen_deg_made"), sem("gen_deg_added"))
        gen_zeroed, gen_hot, gen_made, gen_added = sem("gen_zeroed"), sem("gen_hot"), sem("gen_made"), sem("gen_added")
        gen_adj_done, gen_rest_done, gen_moved_on = sem("gen_adj_done"), sem("gen_rest_done"), sem("gen_moved_on")
        gen_fix_made, gen_fix_added = sem("gen_fix_made"), sem("gen_fix_added")

        block = ctx.enter_context(nc.Block())

        @block.sync
        def _(sp):
            sp.dma_start(dst_all[:, :], dst.rearrange("(p k) -> p k", p=ROWS)).then_inc(dst_in, 16)

            sp.dma_start(src_all[:, :], src.rearrange("(p k) -> p k", p=ROWS)).then_inc(src_in, 16)

            def load_x(t):
                sp.dma_start(x_all[:, t, :], x[t * ROWS:(t + 1) * ROWS, :]).then_inc(x_in[t], 16)

            load_x(0)
            sp.dma_start(wn_raw[:, :, :], w_neigh_t.rearrange("(k p) n -> p k n", p=128)).then_inc(wn_in, 16)
            load_x(1)
            sp.dma_start(ws_raw[:, :, :], w_self_t.rearrange("(k p) n -> p k n", p=128)).then_inc(ws_in, 16)
            load_x(2)
            for row, to in ((b_neigh, bneigh), (b_self, bself), (beta, bet), (gamma, gam), (b2, b2_bc)):
                sp.dma_start(to[:, :], row.partition_broadcast(ROWS)).then_inc(bias_in, 16)
            for t in range(3, 5):
                load_x(t)
            sp.dma_start(w1_raw[:, :, :], w1_t.rearrange("(k p) n -> p k n", p=128)).then_inc(w1_in, 16)
            sp.dma_start(wr_raw[:, :, :], router_t.rearrange("(k p) n -> p k n", p=128)).then_inc(wr_in, 16)
            sp.dma_start(w2_raw[:, :, :], w2_t.rearrange("(k p) n -> p k n", p=128)).then_inc(w2_in, 16)
            sp.dma_start(b1_col[:, :], b1[:, :]).then_inc(w1_in, 16)
            for t in range(5, TILES):
                load_x(t)
            for t in range(TILES):
                for q in range(PER_TILE):
                    sp.wait_ge(counts_staged, PER_TILE * t + q + 1)
                    sp.dma_start(adj[GROUP * q:GROUP * (q + 1), t, :].rearrange("p (f n) -> p f n", f=FIFTHS),
                                 count_stage[:, q, :]).then_inc(counts_moved[q], 16)
            for i in range(TILES):
                sp.wait_ge(out_done, i + 1)
                sp.dma_start(out[i * ROWS:(i + 1) * ROWS, :], s_all[:, i, :]).then_inc(stored, 16)
            sp.wait_ge(stored, 16 * TILES)
            sp.wait_ge(src_in, 16)

        @block.gpsimd
        def _(pool):
            steps = [0]

            def chain(ins):
                steps[0] += 1
                ins.then_inc(pool_step, 1)
                pool.wait_ge(pool_step, steps[0])

            pool.iota(bounds[:, :], [[GROUP, GROUPS]], base=0, channel_multiplier=0,
                      allow_small_or_imprecise_dtypes=True).then_inc(const_done, 1)
            pool.memset(minus_half[:, :], -0.5).then_inc(const_done, 1)
            pool.memset(onesf[:, :], 1.0).then_inc(const_done, 1)
            chain(pool.memset(ident[:, :], 0.0))
            pool.affine_select(out=ident[:, :], in_=ident[:, :], compare_op=ALU.not_equal, fill=1.0, base=0,
                               pattern=[[-1, 128]], channel_multiplier=1).then_inc(const_done, 1)
            pool.iota(base_col[:, :], [[0, 1]], base=0, channel_multiplier=GROUP,
                      allow_small_or_imprecise_dtypes=True).then_inc(const_done, 1)
            pool.wait_ge(const_done, 5)

            def inv_std(var_sem, rstd_sem, mean_var, v_e, r, t):
                pool.wait_ge(var_sem, t + 1)
                chain(pool.tensor_scalar(v_e[:, t % 2, :], mean_var[:, t % 2, 1:2], LN_EPS, None, ALU.add))
                pool.tensor_tensor(r[:, t % 2, :], v_e[:, t % 2, :], minus_half[:, 0:1], ALU.pow).then_inc(rstd_sem, 1)

            inv_std(var_done, rstd_done, mv, ve, rstd, 0)
            pool.iota(iota[:, :], [[1, N_NODES + 1]], base=0, channel_multiplier=0,
                      allow_small_or_imprecise_dtypes=True).then_inc(const_done, 1)
            pool.wait_ge(start_done, 1)
            pool.indirect_dma_start(win_i, None, windows[:, :],
                                    bass.IndirectOffsetOnAxis(start_u[:, 0:1], 0)).then_inc(win_in, 16)
            inv_std(var_done, rstd_done, mv, ve, rstd, 1)
            chain(pool.memset(ones[:, :], 1.0))
            pool.affine_select(out=earlier[:, :], in_=ones[:, :], compare_op=ALU.is_gt, fill=0.0, base=0,
                               pattern=[[1, ROWS]], channel_multiplier=-1).then_inc(const_done, 1)
            pool.memset(chosen_sum[:, :], 0.0).then_inc(const_done, 1)
            pool.wait_ge(bias_in, 80)
            for t in range(TILES):
                if t + 2 < TILES:
                    inv_std(var_done, rstd_done, mv, ve, rstd, t + 2)
                pool.wait_ge(h_done, t + 1)
                pool.tensor_tensor(x_all[:, t, :], x_all[:, t, :], bet[:, :], ALU.add).then_inc(xb_done, 1)
                pool.wait_ge(g_hi_done, t + 1)
                pool.tensor_tensor(g_lo[:, t, :], g_f[:, t % 2, :], g_hi[:, t, :], ALU.subtract).then_inc(g_lo_done, 1)
                pool.wait_ge(s_raw_done, t + 1)
                pool.tensor_tensor(s_all[:, t, :], s_all[:, t, :], bself[:, :], ALU.add).then_inc(s_done, 1)

            def gnn_out(i):
                pool.wait_ge(n1_done, i + 1)
                chain(pool.tensor_tensor(n1g[:, i % 2, :], n1[:, i % 2, :], gam[:, :], ALU.mult))
                pool.tensor_tensor(x_all[:, i, :], n1g[:, i % 2, :], x_all[:, i, :], ALU.add).then_inc(x2_done, 1)

            def gated_bias(i):
                pool.wait_ge(gate_done, i // 2 + 1)
                if i >= 2:
                    pool.wait_ge(out_done, i - 1)
                chain(pool.tensor_scalar(b2g[:, i % 2, :], b2_bc[:, :], gate[:, i % 2, :], None, ALU.mult))
                pool.tensor_tensor(x2b[:, i % 2, :], b2g[:, i % 2, :], x_all[:, i, :], ALU.add).then_inc(x2b_done, 1)

            for j in range(-1, PAIRS + 1):
                a = 2 * (j + 1)
                if j >= 1:
                    gated_bias(2 * j - 2)
                    gated_bias(2 * j - 1)
                if a < TILES:
                    for i in (a, a + 1):
                        inv_std(var1_done, rstd1_done, mv1, ve1, rstd1, i)
                        gnn_out(i)
                        inv_std(var2_done, rstd2_done, mv2, ve2, rstd2, i)

        @block.scalar
        def _(act):
            def split_hi(raw, hi, into):
                act.activation(hi[:], raw[:], ACT.Copy, scale=SW).then_inc(w_hi_done, 1)

            act.wait_ge(wn_in, 16)
            split_hi(wn_raw, wn_hi, 0)

            def stage_counts(g):
                t, q = divmod(g, PER_TILE)
                act.wait_ge(counts_made, g + 1)
                if t >= 1:
                    act.wait_ge(counts_moved[q], 16 * t)
                act.activation(count_stage[:, q, :], p_A[g % 2][0:ROWS, 0:FIFTH], ACT.Copy).then_inc(counts_staged, 1)

            for t in range(TILES + 1):
                g0 = PER_TILE * (t - 1)
                if t < TILES:
                    act.wait_ge(hT_made, t + 1)
                    if t >= 2:
                        act.wait_ge(s_made, t - 1)
                    act.activation(hT_hi[:, t % 2, :, :], p_T[:, 0:KC * ROWS], ACT.Copy, scale=SH).then_inc(hT_hi_done, 1)
                if t == 0:
                    act.wait_ge(ws_in, 16)
                    split_hi(ws_raw, ws_hi, 1)
                if t >= 1:
                    stage_counts(g0)
                    stage_counts(g0 + 1)
                if t < TILES:
                    act.wait_ge(g_f_done, t + 1)
                    act.activation(g_hi[:, t, :], g_f[:, t % 2, :], ACT.Copy).then_inc(g_hi_done, 1)
                if t >= 1:
                    stage_counts(g0 + 2)
                    stage_counts(g0 + 3)
                if t < TILES:
                    act.wait_ge(s_made, t + 1)
                    act.activation(s_all[:, t, :], p_S[0:ROWS, :], ACT.Copy, scale=1.0 / (SH * SW)).then_inc(s_raw_done, 1)
                if t >= 1:
                    stage_counts(g0 + 4)
                if t == 2:
                    act.wait_ge(w1_in, 32)
                    split_hi(w1_raw, w1_hi, 2)
                if t == 3:
                    act.wait_ge(wr_in, 16)
                    split_hi(wr_raw, wr_hi, 3)
                if t == 4:
                    act.wait_ge(w2_in, 16)
                    split_hi(w2_raw, w2_hi, 4)

            for j in range(PAIRS):
                for i in (2 * j, 2 * j + 1):
                    act.wait_ge(xT_made, i + 1)
                    if j >= 1:
                        act.wait_ge(hid_made, j)
                    act.activation(xT_hi[:, :, i % 2, :], p_T[:, 0:KC * ROWS].rearrange("p (k n) -> p k n", k=KC),
                                   ACT.Copy, scale=SH).then_inc(xT_hi_done, 1)
                act.wait_ge(shifted_done, j + 1)
                act.activation(expd[:, :, :], shifted[:, :, :], ACT.Exp).then_inc(exp_done, 1)
                act.wait_ge(hid_made, j + 1)
                if j >= 1:
                    act.wait_ge(hid_done, j)
                for k in range(FC):
                    ins = act.activation(hid[:, k, :], p_H[:, 2 * ROWS * k:2 * ROWS * (k + 1)], ACT.Gelu,
                                         bias=b1_col[:, k:k + 1], scale=1.0 / (SH * SW))
                ins.then_inc(gelu_done, 1)

        @block.tensor
        def _(pe):
            def products(bank_ap, pairs_, n_chunks, made):
                for k in range(n_chunks):
                    for m, (a, b) in enumerate(pairs_):
                        ins = pe.matmul(bank_ap, a(k), b(k), start=(k == 0 and m == 0),
                                        stop=(k == n_chunks - 1 and m == len(pairs_) - 1))
                if made is not None:
                    ins.then_inc(made, 1)

            def turn_h(t):
                pe.wait_ge(h_done, t + 1)
                if t >= 1:
                    pe.wait_ge(hT_lo_done, t)
                for k in range(KC):
                    ins = pe.transpose(p_T[:, ROWS * k:ROWS * (k + 1)], h_all[:, t, 128 * k:128 * (k + 1)],
                                       ident[0:ROWS, 0:ROWS])
                ins.then_inc(hT_made, 1)

            def h_times(t, w_hi, w_lo, bank_, made):
                products(bank_[0:ROWS, :], [(lambda k: hT_hi[:, t % 2, k, :], lambda k: w_hi[:, k, :]),
                                            (lambda k: hT_hi[:, t % 2, k, :], lambda k: w_lo[:, k, :]),
                                            (lambda k: hT_lo[:, t % 2, k, :], lambda k: w_hi[:, k, :])], KC, made)

            def count(g):
                q = g % PER_TILE
                pe.wait_ge(hot_done, g + 1)
                if g >= 2:
                    pe.wait_ge(counts_staged, g - 1)
                for c in range(WCHUNKS):
                    ins = pe.matmul(p_A[g % 2][0:ROWS, 0:FIFTH], hot_row[:, q, c, :], hot_col[:, q, c, :],
                                    start=(c == 0), stop=(c == WCHUNKS - 1))
                ins.then_inc(counts_made, 1)

            def general_counts():
                with pe.Fori(0, ECHUNKS) as c:
                    pe.wait_ge(gen_src_hot, c + 1)
                    for i in range(TILES):
                        ins = pe.matmul(p_R[0:ROWS, i:i + 1], all_src_hot[:, ROWS * i:ROWS * (i + 1)], ones[:, 0:1],
                                        start=True, stop=True)
                    ins.then_inc(gen_deg_made, 1)
                with pe.Fori(0, TILES) as b:
                    with pe.Fori(0, ECHUNKS) as c:
                        pe.wait_ge(gen_hot, b * ECHUNKS + c + 1)
                        for (at, n), to in zip(SRC_PARTS, (p_A0, p_A1, p_S)):
                            ins = pe.matmul(to[0:ROWS, 0:n], all_dst_hot, all_src_hot[:, at:at + n], start=True, stop=True)
                        ins.then_inc(gen_made, 1)
                    pe.wait_ge(gen_rest_done, b + 1)
                    for i in range(TILES):
                        if i >= 1:
                            pe.wait_ge(gen_fix_added, b * TILES + i)
                        src_tile = rest[:, ROWS * i:ROWS * (i + 1)]
                        pe.matmul(p_G[0:ROWS, :], src_tile, g_hi[:, bass.ds(b, 1), :], start=True, stop=False)
                        pe.matmul(p_G[0:ROWS, :], src_tile, g_lo[:, bass.ds(b, 1), :], start=False, stop=True)\
                            .then_inc(gen_fix_made, 1)
                pe.wait_ge(gen_adj_done, TILES)
                pe.wait_ge(gen_fix_added, TILES * TILES)

            pe.wait_ge(const_done, 5)
            pe.wait_ge(below_done, 1)
            pe.matmul(p_R[0:GROUPS, 0:1], below_sum[:, :], onesf[0:ROWS, :], start=True, stop=True).then_inc(start_counted, 1)

            for t in range(TILES + 1):
                g0 = PER_TILE * (t - 1)
                if t < TILES:
                    turn_h(t)
                if t >= 1:
                    count(g0)
                    count(g0 + 1)
                if t < TILES:
                    if t == 0:
                        pe.wait_ge(w_lo_done, 1)
                    pe.wait_ge(hT_lo_done, t + 1)
                    if t >= 1:
                        pe.wait_ge(g_f_done, t)
                    h_times(t, wn_hi, wn_lo, p_G, g_made)
                if t >= 1:
                    count(g0 + 2)
                    count(g0 + 3)
                if t < TILES:
                    if t == 0:
                        pe.wait_ge(w_lo_done, 2)
                    if t >= 1:
                        pe.wait_ge(s_raw_done, t)
                    h_times(t, ws_hi, ws_lo, p_S, s_made)
                if t >= 1:
                    count(g0 + 4)
                if t == 0:
                    pe.wait_ge(keys_done, 1)
                    for n in range(2 * WCHUNKS):
                        kind, c = divmod(n, WCHUNKS)
                        ins = pe.transpose(p_R[:, GROUPS * n:GROUPS * (n + 1)], keys[:, kind, 128 * c:128 * (c + 1)],
                                           ident[0:GROUPS, 0:GROUPS])
                    ins.then_inc(keys_turned, 1)
                    pe.matmul(p_D[0:1, 0:1], n_valid[:, :], onesf[0:GROUPS, :], start=True, stop=True).then_inc(missed_counted, 1)

            for q in range(PER_TILE):
                pe.wait_ge(counts_moved[q], 16 * TILES)
            pe.wait_ge(g_lo_done, TILES)
            pe.wait_ge(w_lo_done, 5)
            pe.wait_ge(const_done, 8)
            pe.wait_ge(missed_done, 1)
            pe.wait_ge(s_raw_done, TILES)
            n_missed = pe.value_load(missed[0:1, 0:1], min_val=0, max_val=N_EDGES)
            with pe.If(n_missed > 0):
                general_counts()

            def neighbours(i):
                src_tile = slice(ROWS * i, ROWS * (i + 1))
                if i < 2:
                    pe.wait_ge(s_raw_done, TILES)
                else:
                    pe.wait_ge(neigh_read, i - 1)
                if i >= 1:
                    pe.wait_ge(deg_read, i)
                for b in range(TILES):
                    pe.matmul(p_N[i % 2][0:ROWS, :], adj[:, b, src_tile], g_hi[:, b, :], start=(b == 0), stop=False)
                    pe.matmul(p_N[i % 2][0:ROWS, :], adj[:, b, src_tile], g_lo[:, b, :], start=False, stop=(b == TILES - 1))
                    ins = pe.matmul(p_D[0:ROWS, i % 2:i % 2 + 1], adj[:, b, src_tile], ones[:, 0:1],
                                    start=(b == 0), stop=(b == TILES - 1))
                ins.then_inc(neigh_made, 1)

            def turn_xn(i):
                pe.wait_ge(xn_done, i + 1)
                if i >= 1:
                    pe.wait_ge(xT_lo_done, i)
                for k in range(KC):
                    ins = pe.transpose(p_T[:, ROWS * k:ROWS * (k + 1)], xn[:, i % 2, 128 * k:128 * (k + 1)],
                                       ident[0:ROWS, 0:ROWS])
                ins.then_inc(xT_made, 1)

            def route(j):
                pe.wait_ge(xT_lo_done, 2 * j + 2)
                if j >= 1:
                    pe.wait_ge(logits_read, j)
                for u in range(2):
                    products(p_R[0:ROWS, EXPERTS * u:EXPERTS * (u + 1)],
                             [(lambda k: xT_hi[:, k, u, :], lambda k: wr_hi[:, k, :]),
                              (lambda k: xT_hi[:, k, u, :], lambda k: wr_lo[:, k, :]),
                              (lambda k: xT_lo[:, k, u, :], lambda k: wr_hi[:, k, :])], KC,
                             logits_made if u == 1 else None)

            def hidden(j):
                if j >= 1:
                    pe.wait_ge(gelu_done, j)
                for f in range(FC):
                    cols = slice(128 * f, 128 * (f + 1))
                    products(p_H[:, 2 * ROWS * f:2 * ROWS * (f + 1)],
                             [(lambda k: w1_hi[:, k, cols], lambda k: xT_hi[:, k, :, :]),
                              (lambda k: w1_hi[:, k, cols], lambda k: xT_lo[:, k, :, :]),
                              (lambda k: w1_lo[:, k, cols], lambda k: xT_hi[:, k, :, :])], KC,
                             hid_made if f == FC - 1 else None)

            def positions(j):
                pe.wait_ge(chosen_done, j + 1)
                if j >= 1:
                    pe.wait_ge(sum_done, j)
                    pe.wait_ge(gate_done, j)
                for u in range(2):
                    to = p_P[0:ROWS, EXPERTS * u:EXPERTS * (u + 1)]
                    pe.matmul(to, ones[:, :], chosen_sum[:, :], start=True, stop=False)
                    if u == 1:
                        pe.matmul(to, ones[:, :], chosen[:, 0, :], start=False, stop=False)
                    ins = pe.matmul(to, earlier[:, :], chosen[:, u, :], start=False, stop=True)
                ins.then_inc(pos_made, 1)

            def ffn_out(i):
                u = i % 2
                pe.wait_ge(hid_done, i // 2 + 1)
                if i >= 1:
                    pe.wait_ge(out_done, i)
                tok = slice(ROWS * u, ROWS * (u + 1))
                products(p_Y[0:ROWS, :], [(lambda k: hid_hi[:, k, tok], lambda k: w2_hi[:, k, :]),
                                          (lambda k: hid_hi[:, k, tok], lambda k: w2_lo[:, k, :]),
                                          (lambda k: hid_lo[:, k, tok], lambda k: w2_hi[:, k, :])], FC, y_made)

            for j in range(-1, PAIRS + 1):
                a, b, c = 2 * (j + 1), 2 * j, 2 * (j - 1)
                if a < TILES:
                    neighbours(a)
                if c >= 0:
                    positions(j - 1)
                if 0 <= b < TILES:
                    turn_xn(b)
                if c >= 0:
                    ffn_out(c)
                if a < TILES:
                    neighbours(a + 1)
                if 0 <= b < TILES:
                    turn_xn(b + 1)
                if c >= 0:
                    ffn_out(c + 1)
                if 0 <= b < TILES:
                    route(j)
                    hidden(j)

        @block.vector
        def _(dve):
            steps = [0]

            def chain(ins):
                steps[0] += 1
                ins.then_inc(dve_step, 1)
                dve.wait_ge(dve_step, steps[0])

            def ts(o, i, s1, s2, op0, op1=None):
                return dve.tensor_scalar(o, i, s1, s2, op0) if op1 is None else dve.tensor_scalar(o, i, s1, s2, op0, op1)

            def stt(o, i0, s, i1, op0, op1):
                return dve.scalar_tensor_tensor(out=o, in0=i0, scalar=s, in1=i1, op0=op0, op1=op1)

            def statistics(src_ap, st, m, done):
                chain(dve.bn_stats(st, src_ap))
                dve.bn_aggr(m, st).then_inc(done, 1)

            def stats_x(t):
                dve.wait_ge(x_in[t], 16)
                if t >= 2:
                    dve.wait_ge(rstd_done, t - 1)
                    dve.wait_ge(h_done, t - 1)
                statistics(x_all[:, t, :], stats[:, t % 2, :], mv[:, t % 2, :], var_done)

            def norm_x(t):
                dve.wait_ge(var_done, t + 1)
                dve.wait_ge(rstd_done, t + 1)
                ts(h_all[:, t, :], x_all[:, t, :], mv[:, t % 2, 0:1], rstd[:, t % 2, :],
                   ALU.subtract, ALU.mult).then_inc(h_done, 1)

            def split_lo(raw, hi, lo, n):
                dve.wait_ge(w_hi_done, n + 1)
                stt(lo[:], raw[:], SW, hi[:], ALU.mult, ALU.subtract).then_inc(w_lo_done, 1)

            dve.wait_ge(dst_in, 16)
            dve.wait_ge(const_done, 5)
            chain(dve.tensor_copy(samples[:, :], dst_all[:, ::ALIGN]))
            chain(dve.tensor_tensor(below[:, :, :], samples[:, :].unsqueeze(1).broadcast_to([ROWS, GROUPS, SAMPLES]),
                                    bounds[:, :].unsqueeze(2).broadcast_to([ROWS, GROUPS, SAMPLES]), ALU.is_lt))
            dve.tensor_reduce(below_sum[:, :], below[:, :, :], AX.X, ALU.add).then_inc(below_done, 1)
            stats_x(0)
            dve.wait_ge(start_counted, 1)
            chain(ts(start_f[:, :], p_R[0:GROUPS, 0:1], -1.0, 0.0, ALU.add, ALU.max))
            ts(start_u[:, :], start_f[:, :], float(STARTS - 1), None, ALU.min).then_inc(start_done, 1)
            norm_x(0)
            split_lo(wn_raw, wn_hi, wn_lo, 0)
            stats_x(1)

            def edge_keys():
                g25 = base_col[:, 0:1]
                dve.wait_ge(win_in, 16)
                chain(dve.tensor_copy(win[:, :, :], win_i.rearrange("p (a b) -> p a b", a=2)))
                s_, d_ = win[:, 0, :], win[:, 1, :]
                chain(ts(local, d_, g25, None, ALU.subtract))
                chain(ts(valid, local, 0.0, None, ALU.is_ge))
                chain(stt(valid, local, float(GROUP), valid, ALU.is_lt, ALU.mult))
                chain(dve.tensor_reduce(n_valid[:, :], valid, AX.X, ALU.add))
                chain(ts(fifth, s_, float(FIFTH), None, ALU.is_ge))
                for f in range(2, FIFTHS):
                    chain(stt(fifth, s_, float(FIFTH * f), fifth, ALU.is_ge, ALU.add))
                chain(stt(keys[:, 1, :], fifth, -float(FIFTH), s_, ALU.mult, ALU.add))
                chain(stt(local, local, float(FIFTHS), fifth, ALU.mult, ALU.add))
                stt(keys[:, 0, :], local, 1.0, valid, ALU.add, ALU.mult).then_inc(keys_done, 1)
                dve.wait_ge(keys_turned, 1)
                dve.tensor_copy(key_col[:, :, :, :], p_R[:, 0:2 * WCHUNKS * GROUPS].rearrange(
                    "p (a c g) -> p a c g", a=2, c=WCHUNKS)).then_inc(key_cols_done, 1)
                dve.wait_ge(missed_counted, 1)
                ts(missed[:, :], p_D[0:1, 0:1], -1.0, float(N_EDGES), ALU.mult, ALU.add).then_inc(missed_done, 1)
                dve.wait_ge(missed_done, 1)
                dve.wait_ge(key_cols_done, 1)

            def one_hots(g):
                q = g % PER_TILE
                if g >= PER_TILE:
                    dve.wait_ge(counts_made, g - PER_TILE + 1)
                for c in range(WCHUNKS):
                    ts(hot_row[:, q, c, :], iota[:, 1:1 + ROWS], key_col[:, 0, c, g:g + 1], None, ALU.is_equal)
                    ins = ts(hot_col[:, q, c, :], iota[:, 0:FIFTH], key_col[:, 1, c, g:g + 1], None, ALU.is_equal)
                ins.then_inc(hot_done, 1)

            for t in range(TILES):
                g0 = PER_TILE * t
                dve.wait_ge(hT_hi_done, t + 1)
                stt(hT_lo[:, t % 2, :, :].rearrange("p k n -> p (k n)"), p_T[:, 0:KC * ROWS], SH,
                    hT_hi[:, t % 2, :, :].rearrange("p k n -> p (k n)"), ALU.mult, ALU.subtract).then_inc(hT_lo_done, 1)
                if t == 0:
                    split_lo(ws_raw, ws_hi, ws_lo, 1)
                    dve.wait_ge(bias_in, 80)
                    chain(ts(bneigh[:, :], bneigh[:, :], SG, None, ALU.mult))
                else:
                    one_hots(g0)
                dve.wait_ge(g_made, t + 1)
                if t >= 2:
                    dve.wait_ge(g_lo_done, t - 1)
                stt(g_f[:, t % 2, :], p_G[0:ROWS, :], SG / (SH * SW), bneigh[:, :], ALU.mult, ALU.add).then_inc(g_f_done, 1)
                if t == 0:
                    norm_x(1)
                    stats_x(2)
                    edge_keys()
                    dve.wait_ge(const_done, 6)
                    one_hots(0)
                one_hots(g0 + 1)
                one_hots(g0 + 2)
                if t > 0 and t + 2 < TILES:
                    stats_x(t + 2)
                if t > 0 and t + 1 < TILES:
                    norm_x(t + 1)
                one_hots(g0 + 3)
                one_hots(g0 + 4)
                if t == 2:
                    split_lo(w1_raw, w1_hi, w1_lo, 2)
                if t == 3:
                    split_lo(wr_raw, wr_hi, wr_lo, 3)
                if t == 4:
                    split_lo(w2_raw, w2_hi, w2_lo, 4)

            dve.wait_ge(s_done, TILES)
            dve.wait_ge(const_done, 8)

            def general_counts():
                for q in range(PER_TILE):
                    dve.wait_ge(counts_moved[q], 16 * TILES)
                dve.wait_ge(src_in, 16)
                dve.wait_ge(w_lo_done, 5)
                dve.tensor_copy(all_src, src_all[:, :]).then_inc(gen_ready, 1)
                ts(all_dst, dst_all[:, :], 1.0, None, ALU.add).then_inc(gen_ready, 1)
                dve.memset(all_deg, 0.0).then_inc(gen_ready, 1)
                dve.wait_ge(gen_ready, 3)
                with dve.Fori(0, ECHUNKS) as c:
                    ts(all_src_hot, iota[0:ROWS, 0:N_NODES], all_src[:, bass.ds(c, 1)], None, ALU.is_equal)\
                        .then_inc(gen_src_hot, 1)
                    dve.wait_ge(gen_deg_made, c + 1)
                    dve.tensor_tensor(all_deg, all_deg, p_R[0:ROWS, 0:TILES], ALU.add).then_inc(gen_deg_added, 1)
                    dve.wait_ge(gen_deg_added, c + 1)
                ts(all_deg, all_deg, 1.0, SG, ALU.max, ALU.mult).then_inc(gen_ready, 1)
                dve.wait_ge(gen_ready, 4)
                dve.reciprocal(all_inv_deg, all_deg).then_inc(gen_ready, 1)
                dve.wait_ge(gen_ready, 5)
                with dve.Fori(0, TILES) as b:
                    dve.memset(all_counts, 0.0).then_inc(gen_zeroed, 1)
                    with dve.Fori(0, ECHUNKS) as c:
                        ts(all_dst_hot, iota[0:ROWS, 1:1 + ROWS], all_dst[:, bass.ds(c, 1)], None, ALU.is_equal)
                        ts(all_src_hot, iota[0:ROWS, 0:N_NODES], all_src[:, bass.ds(c, 1)], None, ALU.is_equal)\
                            .then_inc(gen_hot, 1)
                        dve.wait_ge(gen_zeroed, b + 1)
                        dve.wait_ge(gen_made, b * ECHUNKS + c + 1)
                        for (at, n), part in zip(SRC_PARTS, (p_A0, p_A1, p_S)):
                            ins = dve.tensor_tensor(all_counts[:, at:at + n], all_counts[:, at:at + n],
                                                    part[0:ROWS, 0:n], ALU.add)
                        ins.then_inc(gen_added, 1)
                        dve.wait_ge(gen_added, b * ECHUNKS + c + 1)
                    dve.tensor_copy(adj[:, bass.ds(b, 1), :], all_counts.unsqueeze(1)).then_inc(gen_adj_done, 1)
                    dve.wait_ge(gen_adj_done, b + 1)
                    dve.tensor_tensor(rest.unsqueeze(1), all_counts.unsqueeze(1), adj[:, bass.ds(b, 1), :],
                                      ALU.subtract).then_inc(gen_rest_done, 1)
                    ts(all_dst, all_dst, float(ROWS), None, ALU.subtract).then_inc(gen_moved_on, 1)
                    dve.wait_ge(gen_moved_on, b + 1)
                    for i in range(TILES):
                        dve.wait_ge(gen_fix_made, b * TILES + i + 1)
                        stt(s_all[:, i, :], p_G[0:ROWS, :], all_inv_deg[:, i:i + 1], s_all[:, i, :], ALU.mult, ALU.add)\
                            .then_inc(gen_fix_added, 1)
                        dve.wait_ge(gen_fix_added, b * TILES + i + 1)

            n_missed = dve.value_load(missed[0:1, 0:1], min_val=0, max_val=N_EDGES)
            with dve.If(n_missed > 0):
                general_counts()

            def combine(i):
                u = i % 2
                dve.wait_ge(neigh_made, i + 1)
                ts(deg[:, u, :], p_D[0:ROWS, u:u + 1], 1.0, SG, ALU.max, ALU.mult).then_inc(deg_read, 1)
                dve.wait_ge(deg_read, i + 1)
                chain(dve.reciprocal(inv_deg[:, u, :], deg[:, u, :]))
                stt(relu_in[:, u, :], p_N[u][0:ROWS, :], inv_deg[:, u, :], s_all[:, i, :], ALU.mult, ALU.add).then_inc(neigh_read, 1)
                dve.wait_ge(neigh_read, i + 1)
                chain(stt(x1[:, u, :], relu_in[:, u, :], 0.0, h_all[:, i, :], ALU.max, ALU.add))
                statistics(x1[:, u, :], stats1[:, u, :], mv1[:, u, :], var1_done)

            def norm_1(i):
                u = i % 2
                dve.wait_ge(rstd1_done, i + 1)
                if i >= 2:
                    dve.wait_ge(x2_done, i - 1)
                ts(n1[:, u, :], x1[:, u, :], mv1[:, u, 0:1], rstd1[:, u, :], ALU.subtract, ALU.mult).then_inc(n1_done, 1)

            def stats_2(i):
                dve.wait_ge(x2_done, i + 1)
                statistics(x_all[:, i, :], stats2[:, i % 2, :], mv2[:, i % 2, :], var2_done)

            def norm_2(i):
                u = i % 2
                dve.wait_ge(rstd2_done, i + 1)
                if i >= 2:
                    dve.wait_ge(xT_made, i - 1)
                ts(xn[:, u, :], x_all[:, i, :], mv2[:, u, 0:1], rstd2[:, u, :], ALU.subtract, ALU.mult).then_inc(xn_done, 1)

            def xT_low(i):
                dve.wait_ge(xT_hi_done, i + 1)
                stt(xT_lo[:, :, i % 2, :], p_T[:, 0:KC * ROWS].rearrange("p (k n) -> p k n", k=KC), SH,
                    xT_hi[:, :, i % 2, :], ALU.mult, ALU.subtract).then_inc(xT_lo_done, 1)

            def wide(ap):
                return ap.unsqueeze(2).broadcast_to([ROWS, 2, EXPERTS])

            def softmax_in(j):
                dve.wait_ge(logits_made, j + 1)
                ts(logits[:, :, :], p_R[0:ROWS, 0:2 * EXPERTS].rearrange("p (u e) -> p u e", u=2),
                   1.0 / (SH * SW), None, ALU.mult).then_inc(logits_read, 1)
                dve.wait_ge(logits_read, j + 1)
                chain(dve.tensor_reduce(top[:, :], logits[:, :, :], AX.X, ALU.max))
                dve.tensor_tensor(shifted[:, :, :], logits[:, :, :], wide(top[:, :]), ALU.subtract).then_inc(shifted_done, 1)

            def choose(j):
                dve.wait_ge(exp_done, j + 1)
                chain(dve.tensor_reduce(esum[:, :], expd[:, :, :], AX.X, ALU.add))
                chain(dve.reciprocal(rsum[:, :], esum[:, :]))
                chain(dve.tensor_tensor(probs[:, :, :], expd[:, :, :], wide(rsum[:, :]), ALU.mult))
                for u in range(2):
                    chain(dve.max(best[:, u, :], probs[:, u, :]))
                    chain(dve.max_index(best_at[:, u, :], best[:, u, :], probs[:, u, :]))
                chain(dve.tensor_copy(best_f[:, :, :], best_at[:, :, :]))
                if j >= 1:
                    dve.wait_ge(sum_done, j)
                for u in range(2):
                    chain(ts(first_hot[:, u, :], iota[0:ROWS, 0:EXPERTS], best_f[:, u, 0:1], None, ALU.is_equal))
                for u in range(2):
                    ins = stt(chosen[:, u, :], iota[0:ROWS, 0:EXPERTS], best_f[:, u, 1:2], first_hot[:, u, :],
                              ALU.is_equal, ALU.add)
                ins.then_inc(chosen_done, 1)
                dve.wait_ge(chosen_done, j + 1)
                dve.tensor_tensor(chosen_p[:, :, :], probs[:, :, :], chosen[:, :, :], ALU.mult)

            def gates(j):
                dve.wait_ge(pos_made, j + 1)
                chain(stt(kept_p[:, :, :], p_P[0:ROWS, 0:2 * EXPERTS].rearrange("p (u e) -> p u e", u=2), float(CAPACITY),
                          chosen_p[:, :, :], ALU.is_lt, ALU.mult))
                if j >= 1:
                    dve.wait_ge(x2b_done, 2 * j)
                chain(dve.tensor_reduce(gate[:, :, :], kept_p[:, :, :], AX.X, ALU.add))
                ts(gate_s[:, :, :], gate[:, :, :], 1.0 / (SF * SW), None, ALU.mult).then_inc(gate_done, 1)
                chain(dve.tensor_tensor(chosen_sum[:, :], chosen_sum[:, :], chosen[:, 0, :], ALU.add))
                dve.tensor_tensor(chosen_sum[:, :], chosen_sum[:, :], chosen[:, 1, :], ALU.add).then_inc(sum_done, 1)

            def split_hidden(j):
                dve.wait_ge(gelu_done, j + 1)
                if j >= 1:
                    dve.wait_ge(y_made, 2 * j)
                chain(ts(hid_hi[:, :, :], hid[:, :, :], SF, None, ALU.mult))
                stt(hid_lo[:, :, :], hid[:, :, :], SF, hid_hi[:, :, :], ALU.mult, ALU.subtract).then_inc(hid_done, 1)

            def result(i):
                u = i % 2
                dve.wait_ge(y_made, i + 1)
                dve.wait_ge(gate_done, i // 2 + 1)
                dve.wait_ge(x2b_done, i + 1)
                stt(s_all[:, i, :], p_Y[0:ROWS, :], gate_s[:, u, :], x2b[:, u, :], ALU.mult, ALU.add).then_inc(out_done, 1)

            for j in range(-1, PAIRS + 1):
                a, b, c = 2 * (j + 1), 2 * j, 2 * (j - 1)
                if c >= 0:
                    gates(j - 1)
                if 0 <= b < TILES:
                    xT_low(b)
                if c >= 0:
                    result(c)
                if a < TILES:
                    combine(a)
                if 0 <= b < TILES:
                    xT_low(b + 1)
                if a < TILES:
                    norm_1(a)
                if c >= 0:
                    result(c + 1)
                if a < TILES:
                    stats_2(a)
                    combine(a + 1)
                if 0 <= b < TILES:
                    softmax_in(j)
                if a < TILES:
                    norm_2(a)
                    norm_1(a + 1)
                if 0 <= b < TILES:
                    choose(j)
                if a < TILES:
                    stats_2(a + 1)
                if 0 <= b < TILES:
                    split_hidden(j)
                if a < TILES:
                    norm_2(a + 1)


def kernel(**inputs):
    import concourse.bacc as _bacc
    from concourse.bass_utils import run_bass_kernel_spmd as _run

    src = np.ascontiguousarray(inputs["src"])
    dst = np.ascontiguousarray(inputs["dst"])
    span = WINDOW // ALIGN
    windows = np.concatenate([np.reshape(e, (N_EDGES // ALIGN, ALIGN))[k:k + STARTS]
                              for e in (src, dst) for k in range(span)], axis=1)
    arrays_in = [
        ("x", inputs["x"]), ("windows", windows), ("src", src), ("dst", dst),
        ("w_neigh_t", inputs["L0_gnn_W_neigh"].T), ("w_self_t", inputs["L0_gnn_W_self"].T),
        ("b_neigh", inputs["L0_gnn_b_neigh"]), ("b_self", inputs["L0_gnn_b_self"]),
        ("gamma", inputs["L0_gnn_ln_gamma"]), ("beta", inputs["L0_gnn_ln_beta"]),
        ("router_t", inputs["L0_ffn_router_w"].T), ("w1_t", inputs["L0_ffn_w1"].T), ("b1", np.reshape(inputs["L0_ffn_b1"], (FC, 128)).T),
        ("w2_t", inputs["L0_ffn_w2"].T), ("b2", inputs["L0_ffn_b2"]),
    ]
    nc = _bacc.Bacc("TRN2", target_bir_lowering=False, num_devices=1)
    arrays, args = {}, []
    for name, a in arrays_in:
        a = np.ascontiguousarray(a)
        arrays[f"in_{name}"] = a
        args.append(nc.dram_tensor(f"in_{name}", a.shape, mybir.dt.from_np(a.dtype), kind="ExternalInput").ap())
    args.append(nc.dram_tensor("result", (N_NODES, DIM), mybir.dt.float32, kind="ExternalOutput").ap())
    gnn_ffn(nc, *args)
    r = _run(nc, [arrays], core_ids=[0])
    return r.results[0]["result"]
```

```python
import numpy as np
import concourse.bass as bass
from concourse import mybir
from contextlib import ExitStack

N_NODES, N_EDGES, DIM, FFN, EXPERTS, CAPACITY = 1250, 20000, 512, 256, 64, 512
LN_EPS = 1e-5
ROWS = 125
TILES = N_NODES // ROWS
PAIRS = TILES // 2
KC = DIM // 128
FC = FFN // 128
GROUP = 25
GROUPS = N_NODES // GROUP
PER_TILE = ROWS // GROUP
HOT_SLOTS = 6
BEFORE = [0] + [3] * (TILES - 2) + [0]
AFTER = [2] + [3] * (TILES - 2) + [0]
FIFTHS = 5
FIFTH = N_NODES // FIFTHS
ALIGN = 16
WINDOW = 512
WCHUNKS = WINDOW // 128
STARTS = N_EDGES // ALIGN - WINDOW // ALIGN + 1
SAMPLES = N_EDGES // ALIGN // ROWS
ECHUNKS = N_EDGES // ROWS
SRC_PARTS = [(0, 500), (500, 500), (1000, 250)]
SH, SW, SG, SF = 64.0, 256.0, 64.0, 16.0


def gnn_ffn(nc, x, windows, src, dst, w_neigh_t, w_self_t, b_neigh, b_self, gamma, beta,
            router_t, w1_t, b1, w2_t, b2, out):
    f32, f16, i32, u32 = mybir.dt.float32, mybir.dt.float16, mybir.dt.int32, mybir.dt.uint32
    ALU, ACT, AX = mybir.AluOpType, mybir.ActivationFunctionType, mybir.AxisListType

    with ExitStack() as ctx:
        def sb(name, shape, dt=f32):
            return ctx.enter_context(nc.sbuf_tensor(name, shape, dt))

        def bank(name):
            return ctx.enter_context(nc.psum_tensor(name, [128, 512], f32))

        def sem(name):
            return ctx.enter_context(nc.semaphore(name))

        x_all = sb("x_all", [ROWS, TILES, DIM])
        h_all = sb("h_all", [ROWS, TILES, DIM])
        s_all = sb("s_all", [ROWS, TILES, DIM])
        g_hi = sb("g_hi", [ROWS, TILES, DIM], f16)
        g_lo = sb("g_lo", [ROWS, TILES, DIM], f16)
        adj_flat = sb("adj", [ROWS, TILES * N_NODES], f16)
        adj = adj_flat[:, :].rearrange("p (t n) -> p t n", t=TILES)
        wn_raw = sb("wn_raw", [128, KC, DIM])
        ws_raw = sb("ws_raw", [128, KC, DIM])
        w1_raw = sb("w1_raw", [128, KC, FFN])
        wr_raw = sb("wr_raw", [128, KC, EXPERTS])
        w2_raw = sb("w2_raw", [128, FC, DIM])
        wn_hi, wn_lo = sb("wn_hi", [128, KC, DIM], f16), sb("wn_lo", [128, KC, DIM], f16)
        ws_hi, ws_lo = sb("ws_hi", [128, KC, DIM], f16), sb("ws_lo", [128, KC, DIM], f16)
        w1_hi, w1_lo = sb("w1_hi", [128, KC, FFN], f16), sb("w1_lo", [128, KC, FFN], f16)
        wr_hi, wr_lo = sb("wr_hi", [128, KC, EXPERTS], f16), sb("wr_lo", [128, KC, EXPERTS], f16)
        w2_hi, w2_lo = sb("w2_hi", [128, FC, DIM], f16), sb("w2_lo", [128, FC, DIM], f16)
        bias_raw = sb("bias_raw", [33, 3, DIM])
        bias = sb("bias", [ROWS, 3, DIM], f16)
        sh_all = sb("sh_all", [ROWS, ROWS], f16)
        sf_all = sb("sf_all", [ROWS, ROWS], f16)
        gam = sb("gam", [ROWS, DIM])
        bet = sb("bet", [ROWS, DIM])
        b1_col = sb("b1_col", [128, FC])
        ident = sb("ident", [128, 128])
        iota = sb("iota", [128, N_NODES + 1], f16)
        iota4 = sb("iota4", [128, FIFTH + 1, WCHUNKS], f16)
        earlier = sb("earlier", [ROWS, ROWS], f16)
        ones = sb("ones", [ROWS, ROWS], f16)
        onesf = sb("onesf", [128, 1])
        minus_half = sb("minus_half", [ROWS, 2])
        dst_all = sb("dst_all", [ROWS, N_EDGES // ROWS], i32)
        src_all = sb("src_all", [ROWS, N_EDGES // ROWS], i32)
        samples = sb("samples", [ROWS, SAMPLES])
        bounds = sb("bounds", [ROWS, GROUPS])
        below_sum = sb("below_sum", [ROWS, GROUPS])
        start_f = sb("start_f", [GROUPS, 1])
        start_u = sb("start_u", [GROUPS, 1], u32)
        base_row = sb("base_row", [128, GROUPS, WCHUNKS])
        n_valid = sb("n_valid", [128, 1])
        missed = sb("missed", [1, 1], i32)
        key_col = sb("key_col", [128, 2, GROUPS, WCHUNKS], f16)
        hot_row_flat = sb("hot_row", [128, HOT_SLOTS * WCHUNKS * ROWS], f16)
        hot_col_flat = sb("hot_col", [128, HOT_SLOTS * WCHUNKS * FIFTH], f16)
        hot_row = hot_row_flat[:, :].rearrange("p (q r c) -> p q r c", q=HOT_SLOTS, c=WCHUNKS)
        hot_col = hot_col_flat[:, :].rearrange("p (q r c) -> p q r c", q=HOT_SLOTS, c=WCHUNKS)
        count_flat = sb("count_stage", [ROWS, PER_TILE * FIFTH], f16)
        count_stage = count_flat[:, :].rearrange("p (q n) -> p q n", q=PER_TILE)
        stats = sb("stats", [ROWS, 2, 6])
        mv = sb("mv", [ROWS, 2, 2])
        rstd = sb("rstd", [ROWS, 2, 1])
        ve = sb("ve", [ROWS, 2, 1])
        hT_flat = sb("hT", [128, 2 * 2 * KC * ROWS], f16)
        hT_hi, hT_lo = [hT_flat[:, 2 * KC * ROWS * n:2 * KC * ROWS * (n + 1)].rearrange("p (u k n) -> p u k n", u=2, k=KC)
                        for n in range(2)]
        sum1, neg_mean1, squares1 = sb("sum1", [ROWS, 2, 1]), sb("neg_mean1", [ROWS, 2, 1]), sb("squares1", [ROWS, 2, 1])
        sum2, neg_mean2, squares2 = sb("sum2", [ROWS, 2, 1]), sb("neg_mean2", [ROWS, 2, 1]), sb("squares2", [ROWS, 2, 1])
        square = count_flat[:, 0:2 * DIM].bitcast(f32)
        ve1, rstd1 = sb("ve1", [ROWS, 2, 1]), sb("rstd1", [ROWS, 2, 1])
        ve2, rstd2 = sb("ve2", [ROWS, 2, 1]), sb("rstd2", [ROWS, 2, 1])
        deg = sb("deg", [ROWS, 2, 1])
        inv_deg = sb("inv_deg", [ROWS, 2, 1])
        relu_in = wn_raw[0:ROWS, 0:2, :]
        x1 = wn_raw[0:ROWS, 2:4, :]
        centred = ws_raw[0:ROWS, 0:2, :]
        xn = ws_raw[0:ROWS, 2:4, :]
        xT_flat = sb("xT", [128, 2 * KC * 2 * ROWS], f16)
        xT_hi, xT_lo = [xT_flat[:, KC * 2 * ROWS * n:KC * 2 * ROWS * (n + 1)].rearrange("p (k u n) -> p k u n", k=KC, u=2)
                        for n in range(2)]
        scratch = adj_flat[0:GROUPS, :]

        def edge_words(first, rows, dt):
            part = scratch[:, 2 * WINDOW * first:2 * WINDOW * (first + rows)].bitcast(dt)
            return part.rearrange("p (a b) -> p a b", a=rows) if rows > 1 else part

        win_i = edge_words(0, 2, i32).rearrange("p a b -> p (a b)")
        win = edge_words(2, 2, f32)
        below = adj_flat[:, 18 * WINDOW:18 * WINDOW + 2 * GROUPS * SAMPLES].bitcast(f32).rearrange(
            "p (g s) -> p g s", g=GROUPS)
        turned = xT_flat[:, :].bitcast(f32).rearrange("p (a g c) -> p a g c", g=GROUPS, c=WCHUNKS)
        edges = turned[:, 0:2, :, :]
        local, valid, fifth = [turned[:, 2 + n, :, :] for n in range(3)]
        wn_room = wn_raw[:, :, :].rearrange("p k n -> p (k n)")
        ws_room = ws_raw[:, :, :].rearrange("p k n -> p (k n)")
        all_counts = wn_room[0:ROWS, 0:N_NODES]
        all_src_hot = wn_room[0:ROWS, N_NODES:N_NODES + N_NODES // 2].bitcast(f16)
        all_dst_hot = wn_room[0:ROWS, 1880:1944].bitcast(f16)[:, 0:ROWS]
        rest = ws_room[0:ROWS, 0:N_NODES // 2].bitcast(f16)
        all_src = ws_room[0:ROWS, 640:640 + ECHUNKS]
        all_dst = ws_room[0:ROWS, 800:800 + ECHUNKS]
        all_deg = ws_room[0:ROWS, 960:960 + TILES]
        all_inv_deg = ws_room[0:ROWS, 976:976 + TILES]
        hot_words = hot_row_flat[:, :]
        hid = hot_words[:, 0:4 * FC * ROWS].bitcast(f32).rearrange("p (f n) -> p f n", f=FC)
        hid_hi = hot_words[:, 4 * FC * ROWS:6 * FC * ROWS].rearrange("p (f n) -> p f n", f=FC)
        hid_lo = hot_words[:, 6 * FC * ROWS:8 * FC * ROWS].rearrange("p (f n) -> p f n", f=FC)
        hT_words = hT_flat[0:ROWS, 0:6 * 4 * EXPERTS].bitcast(f32).rearrange("p (a u e) -> p a u e", a=6, u=2)
        logits, shifted, expd, probs, chosen_p, kept_p = [hT_words[:, n, :, :] for n in range(6)]
        top = sb("top", [ROWS, 2])
        esum = sb("esum", [ROWS, 2])
        rsum = sb("rsum", [ROWS, 2])
        best = sb("best", [ROWS, 2, 8])
        best_at = sb("best_at", [ROWS, 2, 8], u32)
        best_f = sb("best_f", [ROWS, 2, 8])
        first_hot = sb("first_hot", [ROWS, 2, EXPERTS], f16)
        chosen = sb("chosen", [ROWS, 2, EXPERTS], f16)
        chosen_sum = sb("chosen_sum", [ROWS, EXPERTS], f16)
        gate = sb("gate", [ROWS, 2, 1])
        gate_s = sb("gate_s", [ROWS, 2, 1])

        p_T, p_G, p_S, p_A0, p_A1, p_R, p_D, p_P = [bank(n) for n in
            ("p_T", "p_G", "p_S", "p_A0", "p_A1", "p_R", "p_D", "p_P")]
        p_A = [p_A0, p_A1]
        p_N = [p_G, p_S]
        p_H, p_Y = p_A0, p_A1

        src_in, affine_in, bias_zeroed = sem("src_in"), sem("affine_in"), sem("bias_zeroed")
        bias_hi_done, bias_done = sem("bias_hi_done"), sem("bias_done")
        dst_in, win_in, bias_in, w1_in, wr_in, w2_in = [sem(n) for n in
            ("dst_in", "win_in", "bias_in", "w1_in", "wr_in", "w2_in")]
        wn_in = [sem(f"wn_in{k}") for k in range(KC)]
        ws_in = [sem(f"ws_in{k}") for k in range(KC)]
        x_in = [sem(f"x_in{t}") for t in range(TILES)]
        const_step, const_done = sem("const_step"), sem("const_done")
        below_done, start_counted, start_done = sem("below_done"), sem("start_counted"), sem("start_done")
        win_f_done, edges_turned, key_cols_done = sem("win_f_done"), sem("edges_turned"), sem("key_cols_done")
        n_valid_done, deg_made = sem("n_valid_done"), sem("deg_made")
        missed_counted, missed_done = sem("missed_counted"), sem("missed_done")
        w_hi_done, w_lo_done = sem("w_hi_done"), sem("w_lo_done")
        dve_step, pool_step = sem("dve_step"), sem("pool_step")
        var_done, rstd_done, h_done, xb_done = sem("var_done"), sem("rstd_done"), sem("h_done"), sem("xb_done")
        hT_made, hT_hi_done, hT_lo_done = sem("hT_made"), sem("hT_hi_done"), sem("hT_lo_done")
        g_made, g_hi_done, g_lo_done = sem("g_made"), sem("g_hi_done"), sem("g_lo_done")
        s_made, s_done = sem("s_made"), sem("s_done")
        hot_done, counts_made, counts_staged = sem("hot_done"), sem("counts_made"), sem("counts_staged")
        counts_moved = [sem(f"counts_moved{q}") for q in range(PER_TILE)]
        neigh_made, deg_read, neigh_read = sem("neigh_made"), sem("deg_read"), sem("neigh_read")
        x1_done, mean1_done, squares1_done, rstd1_done = (sem("x1_done"), sem("mean1_done"), sem("squares1_done"),
                                                          sem("rstd1_done"))
        x2_done, mean2_done, squares2_done, rstd2_done = (sem("x2_done"), sem("mean2_done"), sem("squares2_done"),
                                                          sem("rstd2_done"))
        xn_done, inv_deg_done, centred_done = sem("xn_done"), sem("inv_deg_done"), sem("centred_done")
        xT_made, xT_hi_done, xT_lo_done = sem("xT_made"), sem("xT_hi_done"), sem("xT_lo_done")
        logits_made, logits_read, shifted_done, exp_done = (sem("logits_made"), sem("logits_read"),
                                                           sem("shifted_done"), sem("exp_done"))
        probs_done, best_done, chosen_p_done = sem("probs_done"), sem("best_done"), sem("chosen_p_done")
        chosen_done, sum_done, pos_made, gate_done = sem("chosen_done"), sem("sum_done"), sem("pos_made"), sem("gate_done")
        hid_hi_done = sem("hid_hi_done")
        hid_made, gelu_done, hid_done = sem("hid_made"), sem("gelu_done"), sem("hid_done")
        y_made, out_done, stored = sem("y_made"), sem("out_done"), sem("stored")

        gen_ready, gen_src_hot, gen_deg_made, gen_deg_added = (sem("gen_ready"), sem("gen_src_hot"),
                                                               sem("gen_deg_made"), sem("gen_deg_added"))
        gen_zeroed, gen_hot, gen_made, gen_added = sem("gen_zeroed"), sem("gen_hot"), sem("gen_made"), sem("gen_added")
        gen_adj_done, gen_rest_done, gen_moved_on = sem("gen_adj_done"), sem("gen_rest_done"), sem("gen_moved_on")
        gen_fix_made, gen_fix_added = sem("gen_fix_made"), sem("gen_fix_added")

        block = ctx.enter_context(nc.Block())

        @block.sync
        def _(sp):
            sp.dma_start(dst_all[:, :], dst.rearrange("(p k) -> p k", p=ROWS)).then_inc(dst_in, 16)


            def load_x(t):
                sp.dma_start(x_all[:, t, :], x[t * ROWS:(t + 1) * ROWS, :]).then_inc(x_in[t], 16)

            load_x(0)
            for k in range(KC):
                sp.dma_start(wn_raw[:, k, :], w_neigh_t[128 * k:128 * (k + 1), :]).then_inc(wn_in[k], 16)
            load_x(1)
            for k in range(KC):
                sp.dma_start(ws_raw[:, k, :], w_self_t[128 * k:128 * (k + 1), :]).then_inc(ws_in[k], 16)
            load_x(2)
            sp.wait_ge(win_in, 16)
            for row, to in ((beta, bet), (gamma, gam)):
                sp.dma_start(to[:, :], row.partition_broadcast(ROWS)).then_inc(affine_in, 16)
            load_x(3)
            load_x(4)
            sp.dma_start(w1_raw[:, :, :], w1_t.rearrange("(k p) n -> p k n", p=128)).then_inc(w1_in, 16)
            sp.dma_start(wr_raw[:, :, :], router_t.rearrange("(k p) n -> p k n", p=128)).then_inc(wr_in, 16)
            load_x(5)
            sp.dma_start(w2_raw[:, :, :], w2_t.rearrange("(k p) n -> p k n", p=128)).then_inc(w2_in, 16)
            sp.dma_start(b1_col[:, :], b1[:, :]).then_inc(w1_in, 16)
            for t in range(6, TILES):
                load_x(t)
            sp.dma_start(src_all[:, :], src.rearrange("(p k) -> p k", p=ROWS)).then_inc(src_in, 16)
            for t in range(TILES):
                for q in range(PER_TILE):
                    sp.wait_ge(counts_staged, PER_TILE * t + q + 1)
                    sp.dma_start(adj[GROUP * q:GROUP * (q + 1), t, :].rearrange("p (f n) -> p f n", f=FIFTHS),
                                 count_stage[:, q, :]).then_inc(counts_moved[q], 16)
            for i in range(TILES):
                sp.wait_ge(out_done, i + 1)
                sp.dma_start(out[i * ROWS:(i + 1) * ROWS, :], s_all[:, i, :]).then_inc(stored, 16)
            sp.wait_ge(stored, 16 * TILES)
            sp.wait_ge(src_in, 16)

        @block.gpsimd
        def _(pool):
            steps = [0]

            def chain(ins):
                steps[0] += 1
                ins.then_inc(pool_step, 1)
                pool.wait_ge(pool_step, steps[0])

            pool.iota(bounds[:, :], [[GROUP, GROUPS]], base=0, channel_multiplier=0,
                      allow_small_or_imprecise_dtypes=True).then_inc(const_done, 1)
            pool.memset(minus_half[:, :], -0.5).then_inc(const_done, 1)
            pool.memset(onesf[:, :], 1.0).then_inc(const_done, 1)
            chain(pool.memset(ident[:, :], 0.0))
            pool.affine_select(out=ident[:, :], in_=ident[:, :], compare_op=ALU.not_equal, fill=1.0, base=0,
                               pattern=[[-1, 128]], channel_multiplier=1).then_inc(const_done, 1)
            pool.wait_ge(const_done, 4)

            def inv_std(var_sem, rstd_sem, mean_var, v_e, r, t):
                pool.wait_ge(var_sem, t + 1)
                chain(pool.tensor_scalar(v_e[:, t % 2, :], mean_var[:, t % 2, 1:2], LN_EPS, None, ALU.add))
                pool.tensor_tensor(r[:, t % 2, :], v_e[:, t % 2, :], minus_half[:, 0:1], ALU.pow).then_inc(rstd_sem, 1)

            pool.memset(bias[:, :, :].rearrange("p k n -> p (k n)").bitcast(f32), 0.0).then_inc(bias_zeroed, 1)
            inv_std(var_done, rstd_done, mv, ve, rstd, 0)
            pool.wait_ge(start_done, 1)
            pool.indirect_dma_start(win_i, None, windows[:, :],
                                    bass.IndirectOffsetOnAxis(start_u[:, 0:1], 0)).then_inc(win_in, 16)
            pool.iota(base_row[:, :, :], [[GROUP, GROUPS], [0, WCHUNKS]], base=0, channel_multiplier=0,
                      allow_small_or_imprecise_dtypes=True).then_inc(const_done, 1)
            pool.memset(sh_all[:, :], SH).then_inc(bias_zeroed, 1)
            inv_std(var_done, rstd_done, mv, ve, rstd, 1)
            pool.iota(iota4[:, :, :], [[1, FIFTH + 1], [0, WCHUNKS]], base=0, channel_multiplier=0,
                      allow_small_or_imprecise_dtypes=True).then_inc(const_done, 1)
            inv_std(var_done, rstd_done, mv, ve, rstd, 2)
            pool.memset(sf_all[:, :], SF).then_inc(bias_zeroed, 1)
            chain(pool.memset(ones[:, :], 1.0))
            pool.affine_select(out=earlier[:, :], in_=ones[:, :], compare_op=ALU.is_gt, fill=0.0, base=0,
                               pattern=[[1, ROWS]], channel_multiplier=-1).then_inc(const_done, 1)
            pool.memset(chosen_sum[:, :], 0.0).then_inc(const_done, 1)
            pool.iota(iota[:, :], [[1, N_NODES + 1]], base=0, channel_multiplier=0,
                      allow_small_or_imprecise_dtypes=True).then_inc(const_done, 1)
            pool.wait_ge(affine_in, 32)
            for t in range(TILES):
                if t + 3 < TILES:
                    inv_std(var_done, rstd_done, mv, ve, rstd, t + 3)
                pool.wait_ge(h_done, t + 1)
                pool.tensor_tensor(x_all[:, t, :], x_all[:, t, :], bet[:, :], ALU.add).then_inc(xb_done, 1)

            def inv_std_of_squares(sq_sem, rstd_sem, squares, v_e, r, i):
                pool.wait_ge(sq_sem, i + 1)
                chain(pool.tensor_scalar(v_e[:, i % 2, :], squares[:, i % 2, :], 1.0 / DIM, LN_EPS, ALU.mult, ALU.add))
                pool.tensor_tensor(r[:, i % 2, :], v_e[:, i % 2, :], minus_half[:, 0:1], ALU.pow).then_inc(rstd_sem, 1)

            for i in range(TILES):
                inv_std_of_squares(squares1_done, rstd1_done, squares1, ve1, rstd1, i)
                inv_std_of_squares(squares2_done, rstd2_done, squares2, ve2, rstd2, i)

        @block.scalar
        def _(act):
            for k, row in enumerate((b_neigh, b_self, b2)):
                for r in (0, 32):
                    act.dma_start(bias_raw[r:r + 1, k, :], row.rearrange("(a n) -> a n", a=1)).then_inc(bias_in, 16)
            act.wait_ge(bias_in, 96)
            act.wait_ge(bias_zeroed, 1)
            for r in (32, 0):
                act.activation(bias[r:r + 1, :, :], bias_raw[r:r + 1, :, :], ACT.Copy, scale=SW).then_inc(bias_hi_done, 1)

            def split_hi(raw, hi):
                act.activation(hi, raw, ACT.Copy, scale=SW).then_inc(w_hi_done, 1)

            for k in range(2):
                act.wait_ge(wn_in[k], 16)
                split_hi(wn_raw[:, k, :], wn_hi[:, k, :])

            def turned_high_h(t):
                act.wait_ge(hT_made, t + 1)
                if t >= 2:
                    act.wait_ge(s_made, t - 1)
                act.activation(hT_hi[:, t % 2, :, :], p_T[:, 0:KC * ROWS], ACT.Copy, scale=SH).then_inc(hT_hi_done, 1)

            turned_high_h(0)
            for raw, hi, arrived, ks in ((wn_raw, wn_hi, wn_in, range(2, KC)), (ws_raw, ws_hi, ws_in, range(KC))):
                for k in ks:
                    act.wait_ge(arrived[k], 16)
                    split_hi(raw[:, k, :], hi[:, k, :])

            def stage_counts(g):
                t, q = divmod(g, PER_TILE)
                act.wait_ge(counts_made, g + 1)
                if t >= 1:
                    act.wait_ge(counts_moved[q], 16 * t)
                act.activation(count_stage[:, q, :], p_A[g % 2][0:ROWS, 0:FIFTH], ACT.Copy).then_inc(counts_staged, 1)

            g = 0
            for t in range(TILES):
                act.wait_ge(g_made, t + 1)
                act.activation(g_hi[:, t, :], p_G[0:ROWS, :], ACT.Copy, scale=SG / (SH * SW)).then_inc(g_hi_done, 1)
                for _ in range(BEFORE[t]):
                    stage_counts(g)
                    g += 1
                if t + 1 < TILES:
                    turned_high_h(t + 1)
                act.wait_ge(s_made, t + 1)
                act.activation(s_all[:, t, :], p_S[0:ROWS, :], ACT.Copy, scale=1.0 / (SH * SW)).then_inc(s_done, 1)
                for _ in range(AFTER[t]):
                    stage_counts(g)
                    g += 1
                if t == 1:
                    act.wait_ge(w1_in, 32)
                    split_hi(w1_raw[:], w1_hi[:])
                if t == 2:
                    act.wait_ge(wr_in, 16)
                    split_hi(wr_raw[:], wr_hi[:])
                if t == 3:
                    act.wait_ge(w2_in, 16)
                    split_hi(w2_raw[:], w2_hi[:])

            def turned_high(i):
                act.wait_ge(xT_made, i + 1)
                if i >= 2:
                    act.wait_ge(hid_made, i // 2)
                act.activation(xT_hi[:, :, i % 2, :], p_T[:, 0:KC * ROWS].rearrange("p (k n) -> p k n", k=KC),
                               ACT.Copy, scale=SH).then_inc(xT_hi_done, 1)

            def sum_squares(i, mean_sem, of, neg_mean, to, done):
                act.wait_ge(mean_sem, i + 1)
                act.activation(square[:, :], of, ACT.Square, bias=neg_mean[:, i % 2, :],
                               accum_out=to[:, i % 2, :]).then_inc(done, 1)

            def squares_1(i):
                sum_squares(i, mean1_done, x1[:, i % 2, :], neg_mean1, squares1, squares1_done)

            def squares_2(i):
                sum_squares(i, mean2_done, x_all[:, i, :], neg_mean2, squares2, squares2_done)

            for j in range(-1, PAIRS):
                a, b = 2 * (j + 1), 2 * j
                if b >= 0:
                    turned_high(b)
                    squares_2(b + 1)
                    turned_high(b + 1)
                if a < TILES:
                    squares_1(a)
                if b >= 0:
                    act.wait_ge(shifted_done, j + 1)
                    act.activation(expd[:, :, :], shifted[:, :, :], ACT.Exp).then_inc(exp_done, 1)
                if a < TILES:
                    squares_2(a)
                    squares_1(a + 1)
                if b >= 0:
                    act.wait_ge(hid_made, j + 1)
                    if j >= 1:
                        act.wait_ge(hid_done, j)
                    for k in range(FC):
                        ins = act.activation(hid[:, k, :], p_H[:, 2 * ROWS * k:2 * ROWS * (k + 1)], ACT.Gelu,
                                             bias=b1_col[:, k:k + 1], scale=1.0 / (SH * SW))
                    ins.then_inc(gelu_done, 1)

        @block.tensor
        def _(pe):
            def products(bank_ap, pairs_, n_chunks, made, bias_pair=None):
                if bias_pair is not None:
                    pe.matmul(bank_ap, *bias_pair, start=True, stop=False)
                for k in range(n_chunks):
                    for m, (a, b) in enumerate(pairs_):
                        ins = pe.matmul(bank_ap, a(k), b(k), start=(k == 0 and m == 0 and bias_pair is None),
                                        stop=(k == n_chunks - 1 and m == len(pairs_) - 1))
                if made is not None:
                    ins.then_inc(made, 1)

            def turn_h(t):
                pe.wait_ge(h_done, t + 1)
                if t >= 1:
                    pe.wait_ge(hT_lo_done, t)
                for k in range(KC):
                    ins = pe.transpose(p_T[:, ROWS * k:ROWS * (k + 1)], h_all[:, t, 128 * k:128 * (k + 1)],
                                       ident[0:ROWS, 0:ROWS])
                ins.then_inc(hT_made, 1)

            def h_times(t, w_hi, w_lo, n, bank_, made, first_lo=None):
                to = bank_[0:ROWS, :]
                if first_lo is not None:
                    pe.wait_ge(bias_zeroed, 2)
                    pe.wait_ge(bias_done, 1)
                pe.matmul(to, sh_all[:, :], bias[:, n, :], start=True, stop=False)
                for k in range(KC):
                    if first_lo is not None:
                        pe.wait_ge(w_lo_done, first_lo + k + 1)
                    pe.matmul(to, hT_hi[:, t % 2, k, :], w_hi[:, k, :], start=False, stop=False)
                    pe.matmul(to, hT_hi[:, t % 2, k, :], w_lo[:, k, :], start=False, stop=False)
                    ins = pe.matmul(to, hT_lo[:, t % 2, k, :], w_hi[:, k, :], start=False, stop=(k == KC - 1))
                ins.then_inc(made, 1)

            def count(g):
                q = g % HOT_SLOTS
                pe.wait_ge(hot_done, g + 1)
                if g >= 2:
                    pe.wait_ge(counts_staged, g - 1)
                for c in range(WCHUNKS):
                    ins = pe.matmul(p_A[g % 2][0:ROWS, 0:FIFTH], hot_row[:, q, :, c], hot_col[:, q, :, c],
                                    start=(c == 0), stop=(c == WCHUNKS - 1))
                ins.then_inc(counts_made, 1)

            def general_counts():
                pe.wait_ge(s_done, TILES)
                with pe.Fori(0, ECHUNKS) as c:
                    pe.wait_ge(gen_src_hot, c + 1)
                    for i in range(TILES):
                        ins = pe.matmul(p_R[0:ROWS, i:i + 1], all_src_hot[:, ROWS * i:ROWS * (i + 1)], ones[:, 0:1],
                                        start=True, stop=True)
                    ins.then_inc(gen_deg_made, 1)
                with pe.Fori(0, TILES) as b:
                    with pe.Fori(0, ECHUNKS) as c:
                        pe.wait_ge(gen_hot, b * ECHUNKS + c + 1)
                        for (at, n), to in zip(SRC_PARTS, (p_A0, p_A1, p_S)):
                            ins = pe.matmul(to[0:ROWS, 0:n], all_dst_hot, all_src_hot[:, at:at + n], start=True, stop=True)
                        ins.then_inc(gen_made, 1)
                    pe.wait_ge(gen_rest_done, b + 1)
                    for i in range(TILES):
                        if i >= 1:
                            pe.wait_ge(gen_fix_added, b * TILES + i)
                        src_tile = rest[:, ROWS * i:ROWS * (i + 1)]
                        pe.matmul(p_G[0:ROWS, :], src_tile, g_hi[:, bass.ds(b, 1), :], start=True, stop=False)
                        pe.matmul(p_G[0:ROWS, :], src_tile, g_lo[:, bass.ds(b, 1), :], start=False, stop=True)\
                            .then_inc(gen_fix_made, 1)
                pe.wait_ge(gen_adj_done, TILES)
                pe.wait_ge(gen_fix_added, TILES * TILES)

            pe.wait_ge(const_done, 4)
            pe.wait_ge(below_done, 1)
            pe.matmul(p_R[0:GROUPS, 0:1], below_sum[:, :], onesf[0:ROWS, :], start=True, stop=True).then_inc(start_counted, 1)

            turn_h(0)
            g = 0
            for t in range(TILES):
                pe.wait_ge(hT_lo_done, t + 1)
                if t >= 1:
                    pe.wait_ge(g_lo_done, t)
                h_times(t, wn_hi, wn_lo, 0, p_G, g_made, 0 if t == 0 else None)
                for _ in range(BEFORE[t]):
                    count(g)
                    g += 1
                if t + 1 < TILES:
                    turn_h(t + 1)
                if t >= 1:
                    pe.wait_ge(s_done, t)
                h_times(t, ws_hi, ws_lo, 1, p_S, s_made, KC if t == 0 else None)
                if t == 0:
                    pe.wait_ge(win_f_done, 1)
                    for n in range(2 * WCHUNKS):
                        kind, c = divmod(n, WCHUNKS)
                        ins = pe.transpose(p_R[:, GROUPS * n:GROUPS * (n + 1)], win[:, kind, 128 * c:128 * (c + 1)],
                                           ident[0:GROUPS, 0:GROUPS])
                    ins.then_inc(edges_turned, 1)
                for _ in range(AFTER[t]):
                    count(g)
                    g += 1
                if t == 1:
                    pe.wait_ge(n_valid_done, 1)
                    pe.matmul(p_D[0:1, 0:1], n_valid[:, :], onesf[:, :], start=True, stop=True).then_inc(missed_counted, 1)

            for q in range(PER_TILE):
                pe.wait_ge(counts_moved[q], 16 * TILES)
            pe.wait_ge(g_lo_done, TILES)
            pe.wait_ge(w_lo_done, 2 * KC + 3)
            pe.wait_ge(bias_zeroed, 3)
            pe.wait_ge(bias_done, 1)
            pe.wait_ge(const_done, 9)
            pe.wait_ge(missed_done, 1)
            n_missed = pe.value_load(missed[0:1, 0:1], min_val=0, max_val=N_EDGES)
            with pe.If(n_missed > 0):
                general_counts()

            def neighbours(i):
                src_tile = slice(ROWS * i, ROWS * (i + 1))
                if i >= 1:
                    pe.wait_ge(deg_read, i)
                for b in range(TILES):
                    ins = pe.matmul(p_D[0:ROWS, i % 2:i % 2 + 1], adj[:, b, src_tile], ones[:, 0:1],
                                    start=(b == 0), stop=(b == TILES - 1))
                ins.then_inc(deg_made, 1)
                if i == 1:
                    pe.wait_ge(s_done, TILES)
                if i >= 2:
                    pe.wait_ge(neigh_read, i - 1)
                for b in range(TILES):
                    pe.matmul(p_N[i % 2][0:ROWS, :], adj[:, b, src_tile], g_hi[:, b, :], start=(b == 0), stop=False)
                    ins = pe.matmul(p_N[i % 2][0:ROWS, :], adj[:, b, src_tile], g_lo[:, b, :], start=False,
                                    stop=(b == TILES - 1))
                ins.then_inc(neigh_made, 1)

            def turn_xn(i):
                pe.wait_ge(xn_done, i + 1)
                if i >= 1:
                    pe.wait_ge(xT_lo_done, i)
                for k in range(KC):
                    ins = pe.transpose(p_T[:, ROWS * k:ROWS * (k + 1)], xn[:, i % 2, 128 * k:128 * (k + 1)],
                                       ident[0:ROWS, 0:ROWS])
                ins.then_inc(xT_made, 1)

            def route(j):
                pe.wait_ge(xT_lo_done, 2 * j + 2)
                if j >= 1:
                    pe.wait_ge(logits_read, j)
                for u in range(2):
                    products(p_R[0:ROWS, EXPERTS * u:EXPERTS * (u + 1)],
                             [(lambda k: xT_hi[:, k, u, :], lambda k: wr_hi[:, k, :]),
                              (lambda k: xT_hi[:, k, u, :], lambda k: wr_lo[:, k, :]),
                              (lambda k: xT_lo[:, k, u, :], lambda k: wr_hi[:, k, :])], KC,
                             logits_made if u == 1 else None)

            def hidden(j):
                if j >= 1:
                    pe.wait_ge(gelu_done, j)
                for f in range(FC):
                    cols = slice(128 * f, 128 * (f + 1))
                    products(p_H[:, 2 * ROWS * f:2 * ROWS * (f + 1)],
                             [(lambda k: w1_hi[:, k, cols], lambda k: xT_hi[:, k, :, :]),
                              (lambda k: w1_hi[:, k, cols], lambda k: xT_lo[:, k, :, :]),
                              (lambda k: w1_lo[:, k, cols], lambda k: xT_hi[:, k, :, :])], KC,
                             hid_made if f == FC - 1 else None)

            def positions(j):
                pe.wait_ge(chosen_done, j + 1)
                if j >= 1:
                    pe.wait_ge(sum_done, j)
                    pe.wait_ge(gate_done, j)
                for u in range(2):
                    to = p_P[0:ROWS, EXPERTS * u:EXPERTS * (u + 1)]
                    pe.matmul(to, ones[:, :], chosen_sum[:, :], start=True, stop=False)
                    if u == 1:
                        pe.matmul(to, ones[:, :], chosen[:, 0, :], start=False, stop=False)
                    ins = pe.matmul(to, earlier[:, :], chosen[:, u, :], start=False, stop=True)
                ins.then_inc(pos_made, 1)

            def ffn_out(i):
                u = i % 2
                pe.wait_ge(hid_done, i // 2 + 1)
                if i >= 1:
                    pe.wait_ge(out_done, i)
                tok = slice(ROWS * u, ROWS * (u + 1))
                products(p_Y[0:ROWS, :], [(lambda k: hid_hi[:, k, tok], lambda k: w2_hi[:, k, :]),
                                          (lambda k: hid_hi[:, k, tok], lambda k: w2_lo[:, k, :]),
                                          (lambda k: hid_lo[:, k, tok], lambda k: w2_hi[:, k, :])], FC, y_made,
                         (sf_all[:, :], bias[:, 2, :]))

            for j in range(-1, PAIRS + 1):
                a, b, c = 2 * (j + 1), 2 * j, 2 * (j - 1)
                if 0 <= b < TILES:
                    turn_xn(b)
                if a < TILES:
                    neighbours(a)
                if 0 <= b < TILES:
                    turn_xn(b + 1)
                if c >= 0:
                    positions(j - 1)
                    ffn_out(c)
                if 0 <= b < TILES:
                    route(j)
                if a < TILES:
                    neighbours(a + 1)
                if 0 <= b < TILES:
                    hidden(j)
                if c >= 0:
                    ffn_out(c + 1)

        @block.vector
        def _(dve):
            steps = [0]

            def chain(ins):
                steps[0] += 1
                ins.then_inc(dve_step, 1)
                dve.wait_ge(dve_step, steps[0])

            def ts(o, i, s1, s2, op0, op1=None):
                return dve.tensor_scalar(o, i, s1, s2, op0) if op1 is None else dve.tensor_scalar(o, i, s1, s2, op0, op1)

            def stt(o, i0, s, i1, op0, op1):
                return dve.scalar_tensor_tensor(out=o, in0=i0, scalar=s, in1=i1, op0=op0, op1=op1)

            def statistics(src_ap, st, m, done):
                chain(dve.bn_stats(st, src_ap))
                dve.bn_aggr(m, st).then_inc(done, 1)

            def stats_x(t):
                dve.wait_ge(x_in[t], 16)
                if t >= 2:
                    dve.wait_ge(rstd_done, t - 1)
                    dve.wait_ge(h_done, t - 1)
                statistics(x_all[:, t, :], stats[:, t % 2, :], mv[:, t % 2, :], var_done)

            def norm_x(t):
                dve.wait_ge(var_done, t + 1)
                dve.wait_ge(rstd_done, t + 1)
                ts(h_all[:, t, :], x_all[:, t, :], mv[:, t % 2, 0:1], rstd[:, t % 2, :],
                   ALU.subtract, ALU.mult).then_inc(h_done, 1)

            def split_lo(raw, hi, lo, n):
                dve.wait_ge(w_hi_done, n + 1)
                stt(lo, raw, SW, hi, ALU.mult, ALU.subtract).then_inc(w_lo_done, 1)

            def turned_low_h(t):
                dve.wait_ge(hT_hi_done, t + 1)
                stt(hT_lo[:, t % 2, :, :].rearrange("p k n -> p (k n)"), p_T[:, 0:KC * ROWS], SH,
                    hT_hi[:, t % 2, :, :].rearrange("p k n -> p (k n)"), ALU.mult, ALU.subtract).then_inc(hT_lo_done, 1)

            dve.wait_ge(dst_in, 16)
            dve.wait_ge(const_done, 1)
            chain(dve.tensor_copy(samples[:, :], dst_all[:, ::ALIGN]))
            chain(dve.tensor_tensor(below[:, :, :], samples[:, :].unsqueeze(1).broadcast_to([ROWS, GROUPS, SAMPLES]),
                                    bounds[:, :].unsqueeze(2).broadcast_to([ROWS, GROUPS, SAMPLES]), ALU.is_lt))
            dve.tensor_reduce(below_sum[:, :], below[:, :, :], AX.X, ALU.add).then_inc(below_done, 1)
            stats_x(0)
            dve.wait_ge(start_counted, 1)
            chain(ts(start_f[:, :], p_R[0:GROUPS, 0:1], -1.0, 0.0, ALU.add, ALU.max))
            ts(start_u[:, :], start_f[:, :], float(STARTS - 1), None, ALU.min).then_inc(start_done, 1)
            norm_x(0)
            dve.wait_ge(bias_hi_done, 2)
            stt(bias[32:33, :, :], bias_raw[32:33, :, :], SW, bias[32:33, :, :], ALU.mult, ALU.subtract)\
                .then_inc(bias_done, 1)
            for k in range(2):
                split_lo(wn_raw[:, k, :], wn_hi[:, k, :], wn_lo[:, k, :], k)
            turned_low_h(0)
            for k in range(2, KC):
                split_lo(wn_raw[:, k, :], wn_hi[:, k, :], wn_lo[:, k, :], k)
            stats_x(1)
            for k in range(KC):
                split_lo(ws_raw[:, k, :], ws_hi[:, k, :], ws_lo[:, k, :], KC + k)
                if k == 0:
                    norm_x(1)
            stats_x(2)

            def edges_in():
                dve.wait_ge(win_in, 16)
                dve.tensor_copy(win[:, :, :], win_i.rearrange("p (a b) -> p a b", a=2)).then_inc(win_f_done, 1)

            def edge_keys():
                dve.wait_ge(edges_turned, 1)
                for kind in range(2):
                    n = WCHUNKS * GROUPS * kind
                    ins = dve.tensor_copy(edges[:, kind, :, :], p_R[:, n:n + WCHUNKS * GROUPS].rearrange(
                        "p (c g) -> p g c", c=WCHUNKS))
                chain(ins)
                s_, d_ = edges[:, 0, :, :], edges[:, 1, :, :]
                dve.wait_ge(const_done, 5)
                chain(dve.tensor_tensor(local[:, :, :], d_, base_row[:, :, :], ALU.subtract))
                ts(fifth[:, :, :], s_, float(FIFTH), None, ALU.is_ge)
                chain(ts(valid[:, :, :], local[:, :, :], 0.0, None, ALU.is_ge))
                chain(stt(fifth[:, :, :], s_, 2.0 * FIFTH, fifth[:, :, :], ALU.is_ge, ALU.add))
                chain(stt(valid[:, :, :], local[:, :, :], float(GROUP), valid[:, :, :], ALU.is_lt, ALU.mult))
                chain(stt(fifth[:, :, :], s_, 3.0 * FIFTH, fifth[:, :, :], ALU.is_ge, ALU.add))
                dve.tensor_reduce(n_valid[:, :], valid[:, :, :].rearrange("p g c -> p (g c)"), AX.X, ALU.add)\
                    .then_inc(n_valid_done, 1)
                chain(stt(fifth[:, :, :], s_, 4.0 * FIFTH, fifth[:, :, :], ALU.is_ge, ALU.add))
                stt(key_col[:, 1, :, :], fifth[:, :, :], -float(FIFTH), s_, ALU.mult, ALU.add).then_inc(key_cols_done, 1)
                chain(stt(local[:, :, :], local[:, :, :], float(FIFTHS), fifth[:, :, :], ALU.mult, ALU.add))
                stt(key_col[:, 0, :, :], local[:, :, :], 1.0, valid[:, :, :], ALU.add, ALU.mult).then_inc(key_cols_done, 1)
                dve.wait_ge(key_cols_done, 2)
                dve.wait_ge(const_done, 6)

            def one_hots(g):
                q = g % HOT_SLOTS
                if g >= HOT_SLOTS:
                    dve.wait_ge(counts_made, g - HOT_SLOTS + 1)
                for hot, n, first, kind in ((hot_row, ROWS, 1, 0), (hot_col, FIFTH, 0, 1)):
                    ins = dve.tensor_tensor(hot[:, q, :, :], iota4[:, first:first + n, :],
                                            key_col[:, kind, g:g + 1, :].broadcast_to([128, n, WCHUNKS]), ALU.is_equal)
                ins.then_inc(hot_done, 1)

            def message_low(t):
                dve.wait_ge(g_hi_done, t + 1)
                stt(g_lo[:, t, :], p_G[0:ROWS, :], SG / (SH * SW), g_hi[:, t, :], ALU.mult, ALU.subtract).then_inc(g_lo_done, 1)

            edges_in()
            message_low(0)
            turned_low_h(1)
            norm_x(2)
            edge_keys()
            g = 0
            for _ in range(5):
                one_hots(g)
                g += 1
            stats_x(3)
            for t in range(1, TILES):
                for _ in range(AFTER[t] if t + 1 < TILES else 0):
                    one_hots(g)
                    g += 1
                if t + 2 < TILES:
                    norm_x(t + 2)
                message_low(t)
                if t + 1 < TILES:
                    for n in range(BEFORE[t + 1]):
                        one_hots(g)
                        g += 1
                        if n == 0:
                            turned_low_h(t + 1)
                    if BEFORE[t + 1] == 0:
                        turned_low_h(t + 1)
                if t + 3 < TILES:
                    stats_x(t + 3)
                if t == 1:
                    split_lo(w1_raw[:], w1_hi[:], w1_lo[:], 2 * KC)
                if t == 2:
                    split_lo(wr_raw[:], wr_hi[:], wr_lo[:], 2 * KC + 1)
                    dve.wait_ge(missed_counted, 1)
                    ts(missed[:, :], p_D[0:1, 0:1], -1.0, float(N_EDGES), ALU.mult, ALU.add).then_inc(missed_done, 1)
                if t == 3:
                    split_lo(w2_raw[:], w2_hi[:], w2_lo[:], 2 * KC + 2)
            assert g == GROUPS
            dve.wait_ge(missed_done, 1)

            dve.wait_ge(s_done, TILES)
            dve.wait_ge(const_done, 9)
            dve.wait_ge(xb_done, TILES)

            def general_counts():
                for q in range(PER_TILE):
                    dve.wait_ge(counts_moved[q], 16 * TILES)
                dve.wait_ge(src_in, 16)
                dve.wait_ge(w_lo_done, 2 * KC + 3)
                dve.tensor_copy(all_src, src_all[:, :]).then_inc(gen_ready, 1)
                ts(all_dst, dst_all[:, :], 1.0, None, ALU.add).then_inc(gen_ready, 1)
                dve.memset(all_deg, 0.0).then_inc(gen_ready, 1)
                dve.wait_ge(gen_ready, 3)
                with dve.Fori(0, ECHUNKS) as c:
                    ts(all_src_hot, iota[0:ROWS, 0:N_NODES], all_src[:, bass.ds(c, 1)], None, ALU.is_equal)\
                        .then_inc(gen_src_hot, 1)
                    dve.wait_ge(gen_deg_made, c + 1)
                    dve.tensor_tensor(all_deg, all_deg, p_R[0:ROWS, 0:TILES], ALU.add).then_inc(gen_deg_added, 1)
                    dve.wait_ge(gen_deg_added, c + 1)
                ts(all_deg, all_deg, 1.0, SG, ALU.max, ALU.mult).then_inc(gen_ready, 1)
                dve.wait_ge(gen_ready, 4)
                dve.reciprocal(all_inv_deg, all_deg).then_inc(gen_ready, 1)
                dve.wait_ge(gen_ready, 5)
                with dve.Fori(0, TILES) as b:
                    dve.memset(all_counts, 0.0).then_inc(gen_zeroed, 1)
                    with dve.Fori(0, ECHUNKS) as c:
                        ts(all_dst_hot, iota[0:ROWS, 1:1 + ROWS], all_dst[:, bass.ds(c, 1)], None, ALU.is_equal)
                        ts(all_src_hot, iota[0:ROWS, 0:N_NODES], all_src[:, bass.ds(c, 1)], None, ALU.is_equal)\
                            .then_inc(gen_hot, 1)
                        dve.wait_ge(gen_zeroed, b + 1)
                        dve.wait_ge(gen_made, b * ECHUNKS + c + 1)
                        for (at, n), part in zip(SRC_PARTS, (p_A0, p_A1, p_S)):
                            ins = dve.tensor_tensor(all_counts[:, at:at + n], all_counts[:, at:at + n],
                                                    part[0:ROWS, 0:n], ALU.add)
                        ins.then_inc(gen_added, 1)
                        dve.wait_ge(gen_added, b * ECHUNKS + c + 1)
                    dve.tensor_copy(adj[:, bass.ds(b, 1), :], all_counts.unsqueeze(1)).then_inc(gen_adj_done, 1)
                    dve.wait_ge(gen_adj_done, b + 1)
                    dve.tensor_tensor(rest.unsqueeze(1), all_counts.unsqueeze(1), adj[:, bass.ds(b, 1), :],
                                      ALU.subtract).then_inc(gen_rest_done, 1)
                    ts(all_dst, all_dst, float(ROWS), None, ALU.subtract).then_inc(gen_moved_on, 1)
                    dve.wait_ge(gen_moved_on, b + 1)
                    for i in range(TILES):
                        dve.wait_ge(gen_fix_made, b * TILES + i + 1)
                        stt(s_all[:, i, :], p_G[0:ROWS, :], all_inv_deg[:, i:i + 1], s_all[:, i, :], ALU.mult, ALU.add)\
                            .then_inc(gen_fix_added, 1)
                        dve.wait_ge(gen_fix_added, b * TILES + i + 1)

            n_missed = dve.value_load(missed[0:1, 0:1], min_val=0, max_val=N_EDGES)
            with dve.If(n_missed > 0):
                general_counts()

            def degree(i):
                u = i % 2
                dve.wait_ge(deg_made, i + 1)
                ts(deg[:, u, :], p_D[0:ROWS, u:u + 1], 1.0, SG, ALU.max, ALU.mult).then_inc(deg_read, 1)

            def inverse_degree(i):
                dve.wait_ge(deg_read, i + 1)
                dve.reciprocal(inv_deg[:, i % 2, :], deg[:, i % 2, :]).then_inc(inv_deg_done, 1)

            def before_relu(i):
                u = i % 2
                dve.wait_ge(neigh_made, i + 1)
                dve.wait_ge(inv_deg_done, i + 1)
                stt(relu_in[:, u, :], p_N[u][0:ROWS, :], inv_deg[:, u, :], s_all[:, i, :], ALU.mult, ALU.add).then_inc(neigh_read, 1)

            def residual(i):
                u = i % 2
                dve.wait_ge(neigh_read, i + 1)
                dve.scalar_tensor_tensor(out=x1[:, u, :], in0=relu_in[:, u, :], scalar=0.0, in1=h_all[:, i, :],
                                         op0=ALU.max, op1=ALU.add, accum_out=sum1[:, u, :]).then_inc(x1_done, 1)

            def mean_1(i):
                dve.wait_ge(x1_done, i + 1)
                ts(neg_mean1[:, i % 2, :], sum1[:, i % 2, :], -1.0 / DIM, None, ALU.mult).then_inc(mean1_done, 1)

            def centre(i):
                u = i % 2
                dve.wait_ge(mean1_done, i + 1)
                stt(centred[:, u, :], x1[:, u, :], neg_mean1[:, u, :], gam[:, :], ALU.add, ALU.mult).then_inc(centred_done, 1)

            def gnn_out(i):
                u = i % 2
                dve.wait_ge(centred_done, i + 1)
                dve.wait_ge(rstd1_done, i + 1)
                dve.scalar_tensor_tensor(out=x_all[:, i, :], in0=centred[:, u, :], scalar=rstd1[:, u, :],
                                         in1=x_all[:, i, :], op0=ALU.mult, op1=ALU.add,
                                         accum_out=sum2[:, u, :]).then_inc(x2_done, 1)

            def mean_2(i):
                dve.wait_ge(x2_done, i + 1)
                ts(neg_mean2[:, i % 2, :], sum2[:, i % 2, :], -1.0 / DIM, None, ALU.mult).then_inc(mean2_done, 1)

            def norm_2(i):
                u = i % 2
                dve.wait_ge(rstd2_done, i + 1)
                if i >= 2:
                    dve.wait_ge(xT_made, i - 1)
                ts(xn[:, u, :], x_all[:, i, :], neg_mean2[:, u, :], rstd2[:, u, :], ALU.add, ALU.mult).then_inc(xn_done, 1)

            def xT_low(i):
                dve.wait_ge(xT_hi_done, i + 1)
                stt(xT_lo[:, :, i % 2, :], p_T[:, 0:KC * ROWS].rearrange("p (k n) -> p k n", k=KC), SH,
                    xT_hi[:, :, i % 2, :], ALU.mult, ALU.subtract).then_inc(xT_lo_done, 1)

            def wide(ap):
                return ap.unsqueeze(2).broadcast_to([ROWS, 2, EXPERTS])

            def softmax_in(j):
                dve.wait_ge(logits_made, j + 1)
                ts(logits[:, :, :], p_R[0:ROWS, 0:2 * EXPERTS].rearrange("p (u e) -> p u e", u=2),
                   1.0 / (SH * SW), None, ALU.mult).then_inc(logits_read, 1)
                dve.wait_ge(logits_read, j + 1)
                chain(dve.tensor_reduce(top[:, :], logits[:, :, :], AX.X, ALU.max))
                dve.tensor_tensor(shifted[:, :, :], logits[:, :, :], wide(top[:, :]), ALU.subtract).then_inc(shifted_done, 1)

            def softmax_out(j):
                dve.wait_ge(exp_done, j + 1)
                chain(dve.tensor_reduce(esum[:, :], expd[:, :, :], AX.X, ALU.add))
                chain(dve.reciprocal(rsum[:, :], esum[:, :]))
                dve.tensor_tensor(probs[:, :, :], expd[:, :, :], wide(rsum[:, :]), ALU.mult).then_inc(probs_done, 1)

            def best_two(j):
                dve.wait_ge(probs_done, j + 1)
                dve.max(best[:, 0, :], probs[:, 0, :])
                chain(dve.max(best[:, 1, :], probs[:, 1, :]))
                dve.max_index(best_at[:, 0, :], best[:, 0, :], probs[:, 0, :])
                dve.max_index(best_at[:, 1, :], best[:, 1, :], probs[:, 1, :]).then_inc(best_done, 1)

            def choose(j):
                dve.wait_ge(best_done, j + 1)
                chain(dve.tensor_copy(best_f[:, :, :], best_at[:, :, :]))
                if j >= 1:
                    dve.wait_ge(sum_done, j)
                ts(first_hot[:, 0, :], iota[0:ROWS, 0:EXPERTS], best_f[:, 0, 0:1], None, ALU.is_equal)
                chain(ts(first_hot[:, 1, :], iota[0:ROWS, 0:EXPERTS], best_f[:, 1, 0:1], None, ALU.is_equal))
                for u in range(2):
                    ins = stt(chosen[:, u, :], iota[0:ROWS, 0:EXPERTS], best_f[:, u, 1:2], first_hot[:, u, :],
                              ALU.is_equal, ALU.add)
                ins.then_inc(chosen_done, 1)

            def chosen_probs(j):
                dve.wait_ge(chosen_done, j + 1)
                dve.tensor_tensor(chosen_p[:, :, :], probs[:, :, :], chosen[:, :, :], ALU.mult).then_inc(chosen_p_done, 1)

            def gates(j):
                dve.wait_ge(chosen_p_done, j + 1)
                dve.wait_ge(pos_made, j + 1)
                chain(stt(kept_p[:, :, :], p_P[0:ROWS, 0:2 * EXPERTS].rearrange("p (u e) -> p u e", u=2), float(CAPACITY),
                          chosen_p[:, :, :], ALU.is_lt, ALU.mult))
                chain(dve.tensor_reduce(gate[:, :, :], kept_p[:, :, :], AX.X, ALU.add))
                ts(gate_s[:, :, :], gate[:, :, :], 1.0 / (SF * SW), None, ALU.mult).then_inc(gate_done, 1)
                chain(dve.tensor_tensor(chosen_sum[:, :], chosen_sum[:, :], chosen[:, 0, :], ALU.add))
                dve.tensor_tensor(chosen_sum[:, :], chosen_sum[:, :], chosen[:, 1, :], ALU.add).then_inc(sum_done, 1)

            def hidden_high(j):
                dve.wait_ge(gelu_done, j + 1)
                if j >= 1:
                    dve.wait_ge(y_made, 2 * j)
                ts(hid_hi[:, :, :], hid[:, :, :], SF, None, ALU.mult).then_inc(hid_hi_done, 1)

            def hidden_low(j):
                dve.wait_ge(hid_hi_done, j + 1)
                stt(hid_lo[:, :, :], hid[:, :, :], SF, hid_hi[:, :, :], ALU.mult, ALU.subtract).then_inc(hid_done, 1)

            def result(i):
                u = i % 2
                dve.wait_ge(y_made, i + 1)
                dve.wait_ge(gate_done, i // 2 + 1)
                stt(s_all[:, i, :], p_Y[0:ROWS, :], gate_s[:, u, :], x_all[:, i, :], ALU.mult, ALU.add).then_inc(out_done, 1)

            for j in range(-1, PAIRS + 2):
                a, b, c, d = 2 * (j + 1), 2 * j, 2 * (j - 1), 2 * (j - 2)
                more, mine, last = a < TILES, 0 <= b < TILES, 0 <= c < TILES
                if mine:
                    gnn_out(b + 1)
                if mine:
                    xT_low(b)
                    mean_2(b + 1)
                if last:
                    hidden_high(j - 1)
                if 0 <= d < TILES:
                    result(d + 1)
                if last:
                    hidden_low(j - 1)
                if mine:
                    norm_2(b + 1)
                if more:
                    degree(a)
                    inverse_degree(a)
                    before_relu(a)
                if mine:
                    xT_low(b + 1)
                if more:
                    residual(a)
                if last:
                    gates(j - 1)
                if more:
                    mean_1(a)
                if last:
                    result(c)
                if more:
                    centre(a)
                if mine:
                    softmax_in(j)
                if more:
                    gnn_out(a)
                if mine:
                    softmax_out(j)
                if more:
                    mean_2(a)
                if mine:
                    best_two(j)
                    choose(j)
                if more:
                    norm_2(a)
                    degree(a + 1)
                if mine:
                    chosen_probs(j)
                if more:
                    inverse_degree(a + 1)
                    before_relu(a + 1)
                    residual(a + 1)
                    mean_1(a + 1)
                    centre(a + 1)



def kernel(**inputs):
    import concourse.bacc as _bacc
    from concourse.bass_utils import run_bass_kernel_spmd as _run

    src = np.ascontiguousarray(inputs["src"])
    dst = np.ascontiguousarray(inputs["dst"])
    span = WINDOW // ALIGN
    windows = np.concatenate([np.reshape(e, (N_EDGES // ALIGN, ALIGN))[k:k + STARTS]
                              for e in (src, dst) for k in range(span)], axis=1)
    arrays_in = [
        ("x", inputs["x"]), ("windows", windows), ("src", src), ("dst", dst),
        ("w_neigh_t", inputs["L0_gnn_W_neigh"].T), ("w_self_t", inputs["L0_gnn_W_self"].T),
        ("b_neigh", inputs["L0_gnn_b_neigh"]), ("b_self", inputs["L0_gnn_b_self"]),
        ("gamma", inputs["L0_gnn_ln_gamma"]), ("beta", inputs["L0_gnn_ln_beta"]),
        ("router_t", inputs["L0_ffn_router_w"].T), ("w1_t", inputs["L0_ffn_w1"].T), ("b1", np.reshape(inputs["L0_ffn_b1"], (FC, 128)).T),
        ("w2_t", inputs["L0_ffn_w2"].T), ("b2", inputs["L0_ffn_b2"]),
    ]
    nc = _bacc.Bacc("TRN2", target_bir_lowering=False, num_devices=1)
    arrays, args = {}, []
    for name, a in arrays_in:
        a = np.ascontiguousarray(a)
        arrays[f"in_{name}"] = a
        args.append(nc.dram_tensor(f"in_{name}", a.shape, mybir.dt.from_np(a.dtype), kind="ExternalInput").ap())
    args.append(nc.dram_tensor("result", (N_NODES, DIM), mybir.dt.float32, kind="ExternalOutput").ap())
    gnn_ffn(nc, *args)
    r = _run(nc, [arrays], core_ids=[0])
    return r.results[0]["result"]
```

```python
import numpy as np
import concourse.bass as bass
from concourse import mybir
from contextlib import ExitStack

N_NODES, N_EDGES, DIM, FFN, EXPERTS, CAPACITY = 1250, 20000, 512, 256, 64, 512
LN_EPS = 1e-5
ROWS = 125
TILES = N_NODES // ROWS
PAIRS = TILES // 2
KC = DIM // 128
FC = FFN // 128
GROUP = 12
PARTS = 10
PART = N_NODES // PARTS
HOT_ROWS = GROUP * PARTS
PER_TILE = -(-ROWS // GROUP)
GROUPS = TILES * PER_TILE
DUOS = GROUPS // 2
QUADS = -(-GROUPS // 4)
QUAD_COLS = 4 * PART
HOT_SLOTS = 6
STAGE_SLOTS = 4
BEFORE = [0, 0, 1, 2, 1, 2, 1, 2, 2, 1]
AFTER = [0, 2, 2, 2, 2, 2, 2, 2, 2, 0]
HIDDEN_STEPS = [slice(0, 2 * ROWS)] * (PAIRS - 1) + [slice(0, ROWS), slice(ROWS, 2 * ROWS)]
WARM = [6, 2, 4]
BIAS_ROWS = 24
ALIGN = 8
WINDOW = 256
WCHUNKS = WINDOW // 128
SUMMED = 2048 // WINDOW
DEG_PARTS = 1 + TILES - SUMMED
STARTS = N_EDGES // ALIGN - WINDOW // ALIGN + 1
SAMPLES = N_EDGES // ALIGN // ROWS
ECHUNKS = N_EDGES // ROWS
ROUND = 1.5 * 2 ** 23
SRC_PARTS = [(0, 500), (500, 500), (1000, 250)]
SH, SW, SG, SF = 64.0, 256.0, 64.0, 16.0


def gnn_ffn(nc, x, windows, src, dst, w_neigh_t, w_self_t, biases, gamma, beta,
            router_t, w1_t, b1, w2_t, counts, out):
    f32, f16, i32, u32 = mybir.dt.float32, mybir.dt.float16, mybir.dt.int32, mybir.dt.uint32
    ALU, ACT, AX = mybir.AluOpType, mybir.ActivationFunctionType, mybir.AxisListType

    counts_dram = counts[:, :]
    rows_dram = counts[:, :].rearrange("g (d n) -> (g d) n", d=GROUP)

    def quad_groups(m):
        return range(4 * m, min(4 * m + 4, GROUPS))

    with ExitStack() as ctx:
        def sb(name, shape, dt=f32):
            return ctx.enter_context(nc.sbuf_tensor(name, shape, dt))

        def bank(name):
            return ctx.enter_context(nc.psum_tensor(name, [128, 512], f32))

        def sem(name):
            return ctx.enter_context(nc.semaphore(name))

        x_all = sb("x_all", [ROWS, TILES, DIM])
        h_all = sb("h_all", [ROWS, TILES, DIM])
        s_all = sb("s_all", [ROWS, TILES, DIM])
        g_hi = sb("g_hi", [ROWS, TILES, DIM], f16)
        g_lo = sb("g_lo", [ROWS, TILES, DIM], f16)
        adj_flat = sb("adj", [ROWS, TILES * N_NODES], f16)
        adj = adj_flat[:, :].rearrange("p (t n) -> p t n", t=TILES)
        wn_raw = sb("wn_raw", [128, KC, DIM])
        ws_raw = sb("ws_raw", [128, KC, DIM])
        w1_raw = sb("w1_raw", [128, KC, FFN])
        wr_raw = sb("wr_raw", [128, KC, EXPERTS])
        w2_raw = sb("w2_raw", [128, FC, DIM])
        wn_hi, wn_lo = sb("wn_hi", [128, KC, DIM], f16), sb("wn_lo", [128, KC, DIM], f16)
        ws_hi, ws_lo = sb("ws_hi", [128, KC, DIM], f16), sb("ws_lo", [128, KC, DIM], f16)
        w1_hi, w1_lo = sb("w1_hi", [128, KC, FFN], f16), sb("w1_lo", [128, KC, FFN], f16)
        wr_hi, wr_lo = sb("wr_hi", [128, KC, EXPERTS], f16), sb("wr_lo", [128, KC, EXPERTS], f16)
        w2_hi, w2_lo = sb("w2_hi", [128, FC, DIM], f16), sb("w2_lo", [128, FC, DIM], f16)
        bias_raw = sb("bias_raw", [BIAS_ROWS, 3 * DIM // BIAS_ROWS])
        bias_halves = sb("bias_halves", [BIAS_ROWS, 2, 3 * DIM // BIAS_ROWS], f16)
        bias = sb("bias", [2, 3, DIM], f16)
        sh_rows = sb("sh_rows", [2, ROWS], f16)
        sf_rows = sb("sf_rows", [2, ROWS], f16)
        gam = sb("gam", [ROWS, DIM])
        bet = sb("bet", [ROWS, DIM])
        b1_col = sb("b1_col", [128, FC])
        ident = sb("ident", [128, 128])
        iota = sb("iota", [128, N_NODES + 1], f16)
        iota4 = sb("iota4", [128, PART + 1, 2 * WCHUNKS], f16)
        earlier = sb("earlier", [ROWS, ROWS], f16)
        ones = sb("ones", [ROWS, ROWS], f16)
        onesf = sb("onesf", [128, 1])
        minus_half = sb("minus_half", [ROWS, 2])
        dst_all = sb("dst_all", [ROWS, N_EDGES // ROWS], i32)
        src_all = sb("src_all", [ROWS, N_EDGES // ROWS], i32)
        samples = sb("samples", [ROWS, SAMPLES], f16)
        bounds = sb("bounds", [ROWS, GROUPS], f16)
        start_f = sb("start_f", [GROUPS, 1])
        start_u = sb("start_u", [GROUPS, 1], u32)
        base_row = sb("base_row", [128, (TILES + 1) * PER_TILE, WCHUNKS])
        n_valid = sb("n_valid", [128, 1])
        missed = sb("missed", [1, 1], i32)
        key_col = sb("key_col", [128, 2, GROUPS, WCHUNKS], f16)
        hot_row_flat = sb("hot_row", [128, HOT_SLOTS * 2 * WCHUNKS * HOT_ROWS], f16)
        hot_col_flat = sb("hot_col", [128, HOT_SLOTS * 2 * WCHUNKS * PART], f16)
        hot_row = hot_row_flat[:, :].rearrange("p (q r c) -> p q r c", q=HOT_SLOTS, c=2 * WCHUNKS)
        hot_col = hot_col_flat[:, :].rearrange("p (q r c) -> p q r c", q=HOT_SLOTS, c=2 * WCHUNKS)
        count_stage = sb("count_stage", [HOT_ROWS, STAGE_SLOTS, QUAD_COLS], f16)
        stats = sb("stats", [ROWS, 2, 6])
        mv = sb("mv", [ROWS, 2, 2])
        rstd = sb("rstd", [ROWS, 2, 1])
        ve = sb("ve", [ROWS, 2, 1])
        hT_flat = sb("hT", [128, 2 * 2 * KC * ROWS], f16)
        hT_hi, hT_lo = [hT_flat[:, 2 * KC * ROWS * n:2 * KC * ROWS * (n + 1)].rearrange("p (u k n) -> p u k n", u=2, k=KC)
                        for n in range(2)]
        sum1, neg_mean1, squares1 = sb("sum1", [ROWS, 2, 1]), sb("neg_mean1", [ROWS, 2, 1]), sb("squares1", [ROWS, 2, 1])
        sum2, neg_mean2, squares2 = sb("sum2", [ROWS, 2, 1]), sb("neg_mean2", [ROWS, 2, 1]), sb("squares2", [ROWS, 2, 1])
        square1, square2 = [w[0:ROWS, :, :].rearrange("p k n -> p (k n)").bitcast(f32).rearrange("p (u n) -> p u n", u=2)
                            for w in (wn_hi, ws_hi)]
        ve1, rstd1 = sb("ve1", [ROWS, 2, 1]), sb("rstd1", [ROWS, 2, 1])
        ve2, rstd2 = sb("ve2", [ROWS, 2, 1]), sb("rstd2", [ROWS, 2, 1])
        sum_of_counts = sb("sum_of_counts", [ROWS, N_NODES], f16)
        deg = sb("deg", [ROWS, TILES])
        inv_deg = sb("inv_deg", [ROWS, TILES])
        relu_in = wn_raw[0:ROWS, 0:2, :]
        x1 = wn_raw[0:ROWS, 2:4, :]
        centred = ws_raw[0:ROWS, 0:2, :]
        xn = ws_raw[0:ROWS, 2:4, :]
        xT_flat = sb("xT", [128, 2 * KC * 2 * ROWS], f16)
        xT_hi, xT_lo = [xT_flat[:, KC * 2 * ROWS * n:KC * 2 * ROWS * (n + 1)].rearrange("p (k u n) -> p k u n", k=KC, u=2)
                        for n in range(2)]
        scratch = adj_flat[0:GROUPS, :]

        def edge_words(first, rows, dt):
            part = scratch[:, 2 * WINDOW * first:2 * WINDOW * (first + rows)].bitcast(dt)
            return part.rearrange("p (a b) -> p a b", a=rows) if rows > 1 else part

        win_i = edge_words(0, 2, i32).rearrange("p a b -> p (a b)")
        win = edge_words(2, 2, f32)
        below = adj_flat[:, 8 * WINDOW:8 * WINDOW + GROUPS * SAMPLES].rearrange("p (g s) -> p g s", g=GROUPS)
        key_words = xT_flat[:, 0:4 * 2 * GROUPS * WCHUNKS].bitcast(f32).rearrange("p (a g c) -> p a g c", g=GROUPS, c=WCHUNKS)
        first_row, tenth, valid, next_row = [key_words[:, n, :, :] for n in range(4)]
        wn_room = wn_raw[:, :, :].rearrange("p k n -> p (k n)")
        ws_room = ws_raw[:, :, :].rearrange("p k n -> p (k n)")
        all_counts = wn_room[0:ROWS, 0:N_NODES]
        all_src_hot = wn_room[0:ROWS, N_NODES:N_NODES + N_NODES // 2].bitcast(f16)
        all_dst_hot = wn_room[0:ROWS, 1880:1944].bitcast(f16)[:, 0:ROWS]
        rest = ws_room[0:ROWS, 0:N_NODES // 2].bitcast(f16)
        all_src = ws_room[0:ROWS, 640:640 + ECHUNKS]
        all_dst = ws_room[0:ROWS, 800:800 + ECHUNKS]
        all_deg = ws_room[0:ROWS, 960:960 + TILES]
        all_inv_deg = ws_room[0:ROWS, 976:976 + TILES]
        hot_words = hot_row_flat[:, :]
        hid = hot_words[:, 0:4 * FC * ROWS].bitcast(f32).rearrange("p (f n) -> p f n", f=FC)
        hid_hi, hid_lo = [hot_col_flat[:, 4 * FC * ROWS * n:4 * FC * ROWS * (n + 1)].rearrange("p (v f n) -> p v f n", v=2, f=FC)
                          for n in range(2)]
        hT_words = hT_flat[0:ROWS, 0:4 * 4 * EXPERTS].bitcast(f32).rearrange("p (a u e) -> p a u e", a=4, u=2)
        expd, probs, chosen_p, kept_p = [hT_words[:, n, :, :] for n in range(4)]
        top = sb("top", [ROWS, 2])
        neg_top = sb("neg_top", [ROWS, 2])
        esum = sb("esum", [ROWS, 2])
        rsum = sb("rsum", [ROWS, 2])
        best = sb("best", [ROWS, 2, 8])
        best_at = sb("best_at", [ROWS, 2, 8], u32)
        best_f = sb("best_f", [ROWS, 2, 8])
        first_hot = sb("first_hot", [ROWS, 2, EXPERTS], f16)
        chosen = sb("chosen", [ROWS, 2, EXPERTS], f16)
        chosen_sum = sb("chosen_sum", [ROWS, EXPERTS], f16)
        gate = sb("gate", [ROWS, 2, 1])
        gate_s = sb("gate_s", [ROWS, 2, 1])

        p_T, p_G, p_S, p_A0, p_A1, p_R, p_D, p_P = [bank(n) for n in
            ("p_T", "p_G", "p_S", "p_A0", "p_A1", "p_R", "p_D", "p_P")]
        p_A = [p_A0, p_A1]
        p_N = [p_G, p_S]
        p_H = [p_A0] * PAIRS + [p_G]
        p_Y = [p_A1, p_D]

        src_in, affine_in, bias_scales_done = sem("src_in"), sem("affine_in"), sem("bias_scales_done")
        bias_hi_done, bias_done, bias_moved = sem("bias_hi_done"), sem("bias_done"), sem("bias_moved")
        dst_in, win_in, bias_in, w1_in, wr_in, w2_in = [sem(n) for n in
            ("dst_in", "win_in", "bias_in", "w1_in", "wr_in", "w2_in")]
        wn_in = [sem(f"wn_in{k}") for k in range(KC)]
        ws_in = [sem(f"ws_in{k}") for k in range(KC)]
        x_in = [sem(f"x_in{t}") for t in range(TILES)]
        const_done = sem("const_done")
        below_done, start_counted, start_done = sem("below_done"), sem("start_counted"), sem("start_done")
        win_f_done, edges_turned, key_cols_done = sem("win_f_done"), sem("edges_turned"), sem("key_cols_done")
        n_valid_done, deg_made, counts_summed = sem("n_valid_done"), sem("deg_made"), sem("counts_summed")
        missed_counted, missed_done = sem("missed_counted"), sem("missed_done")
        w_hi_done, w_lo_done = sem("w_hi_done"), sem("w_lo_done")
        dve_step, pool_step = sem("dve_step"), sem("pool_step")
        var_done, rstd_done, h_done, xb_done = sem("var_done"), sem("rstd_done"), sem("h_done"), sem("xb_done")
        hT_made, hT_hi_done, hT_lo_done = sem("hT_made"), sem("hT_hi_done"), sem("hT_lo_done")
        g_made, g_hi_done, g_lo_done = sem("g_made"), sem("g_hi_done"), sem("g_lo_done")
        s_made, s_done = sem("s_made"), sem("s_done")
        hot_done, counts_made, counts_staged = sem("hot_done"), sem("counts_made"), sem("counts_staged")
        counts_written = [sem(f"counts_written{q}") for q in range(STAGE_SLOTS)]
        counts_in = [sem(f"counts_in{t}") for t in range(TILES)]
        neigh_made, deg_read, neigh_read = sem("neigh_made"), sem("deg_read"), sem("neigh_read")
        x1_done, mean1_done, squares1_done, rstd1_done = (sem("x1_done"), sem("mean1_done"), sem("squares1_done"),
                                                          sem("rstd1_done"))
        x2_done, mean2_done, squares2_done, rstd2_done = (sem("x2_done"), sem("mean2_done"), sem("squares2_done"),
                                                          sem("rstd2_done"))
        xn_done, inv_deg_done, centred_done = sem("xn_done"), sem("inv_deg_done"), sem("centred_done")
        xT_made, xT_hi_done, xT_lo_done = sem("xT_made"), sem("xT_hi_done"), sem("xT_lo_done")
        logits_made, top_done, exp_done = sem("logits_made"), sem("top_done"), sem("exp_done")
        probs_done, best_done, chosen_p_done = sem("probs_done"), sem("best_done"), sem("chosen_p_done")
        chosen_done, sum_done, pos_made, gate_done = sem("chosen_done"), sem("sum_done"), sem("pos_made"), sem("gate_done")
        hid_hi_done = sem("hid_hi_done")
        hid_made, gelu_done, hid_done = sem("hid_made"), sem("gelu_done"), sem("hid_done")
        y_made, out_done, stored = sem("y_made"), sem("out_done"), sem("stored")

        gen_ready, gen_src_hot, gen_deg_made, gen_deg_added = (sem("gen_ready"), sem("gen_src_hot"),
                                                               sem("gen_deg_made"), sem("gen_deg_added"))
        gen_zeroed, gen_hot, gen_made, gen_added = sem("gen_zeroed"), sem("gen_hot"), sem("gen_made"), sem("gen_added")
        gen_adj_done, gen_rest_done, gen_moved_on = sem("gen_adj_done"), sem("gen_rest_done"), sem("gen_moved_on")
        gen_fix_made, gen_fix_added = sem("gen_fix_made"), sem("gen_fix_added")

        block = ctx.enter_context(nc.Block())

        @block.sync
        def _(sp):
            sp.dma_start(dst_all[:, :], dst.rearrange("(p k) -> p k", p=ROWS)).then_inc(dst_in, 16)

            def load_x(t):
                sp.dma_start(x_all[:, t, :], x[t * ROWS:(t + 1) * ROWS, :]).then_inc(x_in[t], 16)

            load_x(0)
            for k in range(KC):
                sp.dma_start(wn_raw[:, k, :], w_neigh_t[128 * k:128 * (k + 1), :]).then_inc(wn_in[k], 16)
            load_x(1)
            for k in range(KC):
                sp.dma_start(ws_raw[:, k, :], w_self_t[128 * k:128 * (k + 1), :]).then_inc(ws_in[k], 16)
            load_x(2)
            sp.wait_ge(bias_done, 1)
            for n in range(2):
                sp.dma_start(bias[n:n + 1, :, :].rearrange("a k n -> a (k n)").rearrange("a (p n) -> a p n", p=BIAS_ROWS),
                             bias_halves[:, n, :]).then_inc(bias_moved, 16)
            sp.wait_ge(win_in, 16)
            for row, to in ((beta, bet), (gamma, gam)):
                sp.dma_start(to[:, :], row.partition_broadcast(ROWS)).then_inc(affine_in, 16)
            load_x(3)
            load_x(4)
            sp.dma_start(w1_raw[:, :, :], w1_t.rearrange("(k p) n -> p k n", p=128)).then_inc(w1_in, 16)
            sp.dma_start(wr_raw[:, :, :], router_t.rearrange("(k p) n -> p k n", p=128)).then_inc(wr_in, 16)
            load_x(5)
            sp.dma_start(w2_raw[:, :, :], w2_t.rearrange("(k p) n -> p k n", p=128)).then_inc(w2_in, 16)
            sp.dma_start(b1_col[:, :], b1[:, :]).then_inc(w1_in, 16)
            for t in range(6, TILES):
                load_x(t)
            sp.dma_start(src_all[:, :], src.rearrange("(p k) -> p k", p=ROWS)).then_inc(src_in, 16)
            tile = 0
            for m in range(QUADS):
                groups = quad_groups(m)
                sp.wait_ge(counts_staged, m + 1)
                sp.dma_start(counts_dram[groups.start:groups.stop].rearrange("g (p n) -> p g n", p=HOT_ROWS),
                             count_stage[:, m % STAGE_SLOTS, 0:PART * len(groups)].rearrange("p (g n) -> p g n", g=len(groups)))\
                    .then_inc(counts_written[m % STAGE_SLOTS], 16)
                while tile < TILES and (4 * m >= PER_TILE * (tile + 1) or m == QUADS - 1):
                    for n in range(PER_TILE * tile // 4, (PER_TILE * (tile + 1) - 1) // 4 + 1):
                        sp.wait_ge(counts_written[n % STAGE_SLOTS], 16 * (n // STAGE_SLOTS + 1))
                    sp.dma_start(adj[:, tile, :], rows_dram[GROUP * PER_TILE * tile:GROUP * PER_TILE * tile + ROWS, :])\
                        .then_inc(counts_in[tile], 16)
                    tile += 1
            for i in range(TILES):
                sp.wait_ge(out_done, i + 1)
                sp.dma_start(out[i * ROWS:(i + 1) * ROWS, :], s_all[:, i, :]).then_inc(stored, 16)
            sp.wait_ge(stored, 16 * TILES)
            sp.wait_ge(src_in, 16)

        @block.gpsimd
        def _(pool):
            steps = [0]

            def chain(ins):
                steps[0] += 1
                ins.then_inc(pool_step, 1)
                pool.wait_ge(pool_step, steps[0])

            pool.iota(bounds[:, :], [[ROWS, TILES], [GROUP, PER_TILE]], base=0, channel_multiplier=0,
                      allow_small_or_imprecise_dtypes=True).then_inc(const_done, 1)
            pool.memset(ones[:, :], 1.0).then_inc(const_done, 1)
            pool.memset(minus_half[:, :], -0.5).then_inc(const_done, 1)
            chain(pool.memset(ident[:, :], 0.0))
            pool.affine_select(out=ident[:, :], in_=ident[:, :], compare_op=ALU.not_equal, fill=1.0, base=0,
                               pattern=[[-1, 128]], channel_multiplier=1).then_inc(const_done, 1)
            pool.wait_ge(const_done, 4)

            def inv_std(var_sem, rstd_sem, mean_var, v_e, r, t):
                pool.wait_ge(var_sem, t + 1)
                chain(pool.tensor_scalar(v_e[:, t % 2, :], mean_var[:, t % 2, 1:2], LN_EPS, None, ALU.add))
                pool.tensor_tensor(r[:, t % 2, :], v_e[:, t % 2, :], minus_half[:, 0:1], ALU.pow).then_inc(rstd_sem, 1)

            pool.memset(onesf[:, :], 1.0).then_inc(const_done, 1)
            pool.memset(sh_rows[:, :], SH).then_inc(bias_scales_done, 1)
            pool.memset(sf_rows[:, :], SF).then_inc(bias_scales_done, 1)
            pool.wait_ge(bias_scales_done, 2)
            inv_std(var_done, rstd_done, mv, ve, rstd, 0)
            pool.wait_ge(start_done, 1)
            pool.indirect_dma_start(win_i, None, windows[:, :],
                                    bass.IndirectOffsetOnAxis(start_u[:, 0:1], 0)).then_inc(win_in, 16)
            pool.iota(base_row[:, :, :], [[PARTS * ROWS, TILES + 1], [PARTS * GROUP, PER_TILE], [0, WCHUNKS]], base=-1,
                      channel_multiplier=0,
                      allow_small_or_imprecise_dtypes=True).then_inc(const_done, 1)
            pool.iota(iota4[:, :, :], [[1, PART + 1], [0, 2 * WCHUNKS]], base=0, channel_multiplier=0,
                      allow_small_or_imprecise_dtypes=True).then_inc(const_done, 1)
            inv_std(var_done, rstd_done, mv, ve, rstd, 1)
            inv_std(var_done, rstd_done, mv, ve, rstd, 2)
            pool.affine_select(out=earlier[:, :], in_=ones[:, :], compare_op=ALU.is_gt, fill=0.0, base=0,
                               pattern=[[1, ROWS]], channel_multiplier=-1).then_inc(const_done, 1)
            pool.memset(chosen_sum[:, :], 0.0).then_inc(const_done, 1)
            pool.iota(iota[:, :], [[1, N_NODES + 1]], base=0, channel_multiplier=0,
                      allow_small_or_imprecise_dtypes=True).then_inc(const_done, 1)
            pool.wait_ge(affine_in, 32)
            for t in range(TILES):
                if t + 3 < TILES:
                    inv_std(var_done, rstd_done, mv, ve, rstd, t + 3)
                pool.wait_ge(h_done, t + 1)
                pool.tensor_tensor(x_all[:, t, :], x_all[:, t, :], bet[:, :], ALU.add).then_inc(xb_done, 1)

            def inv_std_of_squares(sq_sem, rstd_sem, squares, v_e, r, i):
                pool.wait_ge(sq_sem, i + 1)
                chain(pool.tensor_scalar(v_e[:, i % 2, :], squares[:, i % 2, :], 1.0 / DIM, LN_EPS, ALU.mult, ALU.add))
                pool.tensor_tensor(r[:, i % 2, :], v_e[:, i % 2, :], minus_half[:, 0:1], ALU.pow).then_inc(rstd_sem, 1)

            def inv_std_1(i):
                inv_std_of_squares(squares1_done, rstd1_done, squares1, ve1, rstd1, i)

            def inv_std_2(i):
                inv_std_of_squares(squares2_done, rstd2_done, squares2, ve2, rstd2, i)

            for i in range(TILES - 2):
                inv_std_1(i)
                inv_std_2(i)
            inv_std_1(TILES - 2)
            inv_std_1(TILES - 1)
            inv_std_2(TILES - 2)
            inv_std_2(TILES - 1)

        @block.scalar
        def _(act):
            act.dma_start(bias_raw[:, :], biases.rearrange("(p n) -> p n", p=BIAS_ROWS)).then_inc(bias_in, 16)
            act.wait_ge(bias_in, 16)
            act.activation(bias_halves[:, 0, :], bias_raw[:, :], ACT.Copy, scale=SW).then_inc(bias_hi_done, 1)

            def split_hi(raw, hi):
                act.activation(hi, raw, ACT.Copy, scale=SW).then_inc(w_hi_done, 1)

            for k in range(2):
                act.wait_ge(wn_in[k], 16)
                split_hi(wn_raw[:, k, :], wn_hi[:, k, :])

            def turned_high_h(t):
                act.wait_ge(hT_made, t + 1)
                if t >= 2:
                    act.wait_ge(s_made, t - 1)
                act.activation(hT_hi[:, t % 2, :, :], p_T[:, 0:KC * ROWS], ACT.Copy, scale=SH).then_inc(hT_hi_done, 1)

            turned_high_h(0)
            for raw, hi, arrived, ks in ((wn_raw, wn_hi, wn_in, range(2, KC)), (ws_raw, ws_hi, ws_in, range(KC))):
                for k in ks:
                    act.wait_ge(arrived[k], 16)
                    split_hi(raw[:, k, :], hi[:, k, :])

            act.wait_ge(win_in, 16)
            act.activation(win[:, :, :], win_i.rearrange("p (a b) -> p a b", a=2), ACT.Copy).then_inc(win_f_done, 1)

            def stage_counts(m):
                cols = PART * len(quad_groups(m))
                act.wait_ge(counts_made, m + 1)
                if m >= STAGE_SLOTS:
                    act.wait_ge(counts_written[m % STAGE_SLOTS], 16 * (m // STAGE_SLOTS))
                act.activation(count_stage[:, m % STAGE_SLOTS, 0:cols], p_A[m % 2][0:HOT_ROWS, 0:cols], ACT.Copy)\
                    .then_inc(counts_staged, 1)

            m = 0
            for t in range(TILES):
                act.wait_ge(g_made, t + 1)
                act.activation(g_hi[:, t, :], p_G[0:ROWS, :], ACT.Copy, scale=SG / (SH * SW)).then_inc(g_hi_done, 1)
                for _ in range(BEFORE[t]):
                    stage_counts(m)
                    m += 1
                if t + 1 < TILES:
                    turned_high_h(t + 1)
                act.wait_ge(s_made, t + 1)
                act.activation(s_all[:, t, :], p_S[0:ROWS, :], ACT.Copy, scale=1.0 / (SH * SW)).then_inc(s_done, 1)
                for _ in range(AFTER[t]):
                    stage_counts(m)
                    m += 1
                if t == 1:
                    act.wait_ge(w1_in, 32)
                    split_hi(w1_raw[:], w1_hi[:])
                if t == 2:
                    act.wait_ge(wr_in, 16)
                    split_hi(wr_raw[:], wr_hi[:])
                if t == 3:
                    act.wait_ge(w2_in, 16)
                    split_hi(w2_raw[:], w2_hi[:])

            def turned_high(i):
                act.wait_ge(xT_made, i + 1)
                if i >= 2:
                    act.wait_ge(hid_made, i // 2)
                    act.wait_ge(logits_made, i // 2)
                act.activation(xT_hi[:, :, i % 2, :], p_T[:, 0:KC * ROWS].rearrange("p (k n) -> p k n", k=KC),
                               ACT.Copy, scale=SH).then_inc(xT_hi_done, 1)

            def sum_squares(i, mean_sem, of, neg_mean, square, to, done):
                act.wait_ge(mean_sem, i + 1)
                act.activation(square[:, i % 2, :], of, ACT.Square, bias=neg_mean[:, i % 2, :],
                               accum_out=to[:, i % 2, :]).then_inc(done, 1)

            def squares_1(i):
                sum_squares(i, mean1_done, x1[:, i % 2, :], neg_mean1, square1, squares1, squares1_done)

            def squares_2(i):
                sum_squares(i, mean2_done, x_all[:, i, :], neg_mean2, square2, squares2, squares2_done)

            def exponentials(j):
                act.wait_ge(top_done, j + 1)
                if j >= 1:
                    act.wait_ge(probs_done, j)
                for u in range(2):
                    ins = act.activation(expd[:, u, :], p_R[0:ROWS, EXPERTS * u:EXPERTS * (u + 1)], ACT.Exp,
                                         bias=neg_top[:, u:u + 1], scale=1.0 / (SH * SW), accum_out=esum[:, u:u + 1])
                ins.then_inc(exp_done, 1)

            def gelus(n):
                tok, j = HIDDEN_STEPS[n], min(n, PAIRS - 1)
                act.wait_ge(hid_made, n + 1)
                if n >= 1:
                    act.wait_ge(hid_done, min(n, PAIRS - 1))
                for f in range(FC):
                    ins = act.activation(hid[:, f, tok], p_H[n][:, 2 * ROWS * f + tok.start:2 * ROWS * f + tok.stop],
                                         ACT.Gelu, bias=b1_col[:, f:f + 1], scale=1.0 / (SH * SW))
                ins.then_inc(gelu_done, 1)
                act.wait_ge(gelu_done, n + 1)
                if j >= 2:
                    act.wait_ge(y_made, 2 * j - 2)
                act.activation(hid_hi[:, j % 2, :, tok], hid[:, :, tok], ACT.Copy, scale=SF).then_inc(hid_hi_done, 1)

            squares_1(0)
            squares_2(0)
            squares_1(1)
            turned_high(0)
            squares_2(1)
            squares_1(2)
            for j in range(PAIRS - 2):
                b = 2 * j
                squares_2(b + 2)
                if j == 0:
                    turned_high(b + 1)
                squares_1(b + 3)
                exponentials(j)
                squares_2(b + 3)
                turned_high(b + 2)
                gelus(j)
                turned_high(b + 3)
                squares_1(b + 4)
            squares_1(TILES - 1)
            squares_2(TILES - 2)
            gelus(PAIRS - 2)
            squares_2(TILES - 1)
            turned_high(TILES - 2)
            exponentials(PAIRS - 2)
            turned_high(TILES - 1)
            gelus(PAIRS - 1)
            gelus(PAIRS)
            exponentials(PAIRS - 1)

        @block.tensor
        def _(pe):
            def products(bank_ap, pairs_, n_chunks, made, bias_pair=None):
                for k in range(n_chunks):
                    for m, (a, b) in enumerate(pairs_):
                        ins = pe.matmul(bank_ap, a(k), b(k), start=(k == 0 and m == 0),
                                        stop=(k == n_chunks - 1 and m == len(pairs_) - 1 and bias_pair is None))
                if bias_pair is not None:
                    ins = pe.matmul(bank_ap, *bias_pair, start=False, stop=True)
                if made is not None:
                    ins.then_inc(made, 1)

            def turn_h(t):
                pe.wait_ge(h_done, t + 1)
                if t >= 1:
                    pe.wait_ge(hT_lo_done, t)
                for k in range(KC):
                    ins = pe.transpose(p_T[:, ROWS * k:ROWS * (k + 1)], h_all[:, t, 128 * k:128 * (k + 1)],
                                       ident[0:ROWS, 0:ROWS])
                ins.then_inc(hT_made, 1)

            def h_times(t, w_hi, w_lo, n, bank_, made, first_lo=None):
                to = bank_[0:ROWS, :]
                for k in range(KC):
                    if first_lo is not None:
                        pe.wait_ge(w_lo_done, first_lo + k + 1)
                    pe.matmul(to, hT_hi[:, t % 2, k, :], w_hi[:, k, :], start=(k == 0), stop=False)
                    pe.matmul(to, hT_hi[:, t % 2, k, :], w_lo[:, k, :], start=False, stop=False)
                    pe.matmul(to, hT_lo[:, t % 2, k, :], w_hi[:, k, :], start=False, stop=False)
                if first_lo == 0:
                    pe.wait_ge(bias_scales_done, 2)
                    pe.wait_ge(bias_moved, 32)
                pe.matmul(to, sh_rows[:, :], bias[:, n, :], start=False, stop=True).then_inc(made, 1)

            def count(m):
                if m >= 2:
                    pe.wait_ge(counts_staged, m - 1)
                for g in quad_groups(m):
                    duo = g // 2
                    pe.wait_ge(hot_done, duo + 1)
                    for c in range(WCHUNKS):
                        at = WCHUNKS * (g % 2) + c
                        ins = pe.matmul(p_A[m % 2][0:HOT_ROWS, PART * (g % 4):PART * (g % 4 + 1)],
                                        hot_row[:, duo % HOT_SLOTS, :, at], hot_col[:, duo % HOT_SLOTS, :, at],
                                        start=(c == 0), stop=(c == WCHUNKS - 1))
                ins.then_inc(counts_made, 1)

            def general_counts():
                pe.wait_ge(s_done, TILES)
                with pe.Fori(0, ECHUNKS) as c:
                    pe.wait_ge(gen_src_hot, c + 1)
                    for i in range(TILES):
                        ins = pe.matmul(p_R[0:ROWS, i:i + 1], all_src_hot[:, ROWS * i:ROWS * (i + 1)], ones[:, 0:1],
                                        start=True, stop=True)
                    ins.then_inc(gen_deg_made, 1)
                with pe.Fori(0, TILES) as b:
                    with pe.Fori(0, ECHUNKS) as c:
                        pe.wait_ge(gen_hot, b * ECHUNKS + c + 1)
                        for (at, n), to in zip(SRC_PARTS, (p_A0, p_A1, p_S)):
                            ins = pe.matmul(to[0:ROWS, 0:n], all_dst_hot, all_src_hot[:, at:at + n], start=True, stop=True)
                        ins.then_inc(gen_made, 1)
                    pe.wait_ge(gen_rest_done, b + 1)
                    for i in range(TILES):
                        if i >= 1:
                            pe.wait_ge(gen_fix_added, b * TILES + i)
                        src_tile = rest[:, ROWS * i:ROWS * (i + 1)]
                        pe.matmul(p_G[0:ROWS, :], src_tile, g_hi[:, bass.ds(b, 1), :], start=True, stop=False)
                        pe.matmul(p_G[0:ROWS, :], src_tile, g_lo[:, bass.ds(b, 1), :], start=False, stop=True)\
                            .then_inc(gen_fix_made, 1)
                pe.wait_ge(gen_adj_done, TILES)
                pe.wait_ge(gen_fix_added, TILES * TILES)

            def part_degrees(n, counts_):
                for i in range(TILES):
                    ins = pe.matmul(p_D[0:ROWS, TILES * n + i:TILES * n + i + 1], counts_[:, ROWS * i:ROWS * (i + 1)],
                                    ones[:, 0:1], start=True, stop=True)
                ins.then_inc(deg_made, 1)

            def keep_warm(n):
                for _ in range(n):
                    pe.matmul(p_S[0:ROWS, :], ones[:, :], ones[:, 0:1].broadcast_to([ROWS, DIM]), start=True, stop=True)

            pe.wait_ge(const_done, 4)
            keep_warm(WARM[0])
            for k in range(SAMPLES):
                if k == SAMPLES // 2:
                    keep_warm(WARM[1])
                pe.wait_ge(below_done, 1 + k // (SAMPLES // 2))
                ins = pe.matmul(p_R[0:GROUPS, 0:1], below[:, :, k], ones[:, 0:1], start=(k == 0), stop=(k == SAMPLES - 1))
            ins.then_inc(start_counted, 1)

            turn_h(0)
            keep_warm(WARM[2])
            m = 0
            for t in range(TILES):
                pe.wait_ge(hT_lo_done, t + 1)
                if t >= 1:
                    pe.wait_ge(g_lo_done, t)
                h_times(t, wn_hi, wn_lo, 0, p_G, g_made, 0 if t == 0 else None)
                for _ in range(BEFORE[t]):
                    count(m)
                    m += 1
                if t == 0:
                    pe.wait_ge(win_f_done, 1)
                    for n in range(2 * WCHUNKS):
                        kind, c = divmod(n, WCHUNKS)
                        ins = pe.transpose(p_R[:, GROUPS * n:GROUPS * (n + 1)], win[:, kind, 128 * c:128 * (c + 1)],
                                           ident[0:GROUPS, 0:GROUPS])
                    ins.then_inc(edges_turned, 1)
                if t + 1 < TILES:
                    turn_h(t + 1)
                if t >= 1:
                    pe.wait_ge(s_done, t)
                h_times(t, ws_hi, ws_lo, 1, p_S, s_made, KC if t == 0 else None)
                for _ in range(AFTER[t]):
                    count(m)
                    m += 1
                if t == 2:
                    pe.wait_ge(n_valid_done, 1)
                    pe.matmul(p_P[0:1, 0:1], n_valid[:, :], onesf[:, :], start=True, stop=True).then_inc(missed_counted, 1)

            pe.wait_ge(w_lo_done, 2 * KC + 3)
            pe.wait_ge(bias_scales_done, 2)
            pe.wait_ge(const_done, 10)
            pe.wait_ge(missed_done, 1)
            n_missed = pe.value_load(missed[0:1, 0:1], min_val=0, max_val=N_EDGES)
            with pe.If(n_missed > 0):
                general_counts()

            def neighbours(i):
                src_tile = slice(ROWS * i, ROWS * (i + 1))
                if i == 0:
                    pe.wait_ge(g_lo_done, TILES)
                if i == 1:
                    pe.wait_ge(s_done, TILES)
                if i >= 2:
                    pe.wait_ge(neigh_read, i - 1)
                for b in range(TILES):
                    if i == 0:
                        pe.wait_ge(counts_in[b], 16)
                    pe.matmul(p_N[i % 2][0:ROWS, :], adj[:, b, src_tile], g_hi[:, b, :], start=(b == 0), stop=False)
                    ins = pe.matmul(p_N[i % 2][0:ROWS, :], adj[:, b, src_tile], g_lo[:, b, :], start=False,
                                    stop=(b == TILES - 1))
                ins.then_inc(neigh_made, 1)

            def turn_xn(i):
                pe.wait_ge(xn_done, i + 1)
                if i >= 1:
                    pe.wait_ge(xT_lo_done, i)
                for k in range(KC):
                    ins = pe.transpose(p_T[:, ROWS * k:ROWS * (k + 1)], xn[:, i % 2, 128 * k:128 * (k + 1)],
                                       ident[0:ROWS, 0:ROWS])
                ins.then_inc(xT_made, 1)

            def route(j):
                pe.wait_ge(xT_lo_done, 2 * j + 2)
                if j >= 1:
                    pe.wait_ge(exp_done, j)
                for u in range(2):
                    products(p_R[0:ROWS, EXPERTS * u:EXPERTS * (u + 1)],
                             [(lambda k: xT_hi[:, k, u, :], lambda k: wr_hi[:, k, :]),
                              (lambda k: xT_hi[:, k, u, :], lambda k: wr_lo[:, k, :]),
                              (lambda k: xT_lo[:, k, u, :], lambda k: wr_hi[:, k, :])], KC,
                             logits_made if u == 1 else None)

            def hidden(n):
                tok = HIDDEN_STEPS[n]
                used = slice(tok.start // ROWS, tok.stop // ROWS)
                pe.wait_ge(xT_lo_done, min(2 * n + 2, TILES))
                if n == PAIRS:
                    pe.wait_ge(neigh_read, TILES - 1)
                elif n >= 1:
                    pe.wait_ge(gelu_done, n)
                for f in range(FC):
                    cols = slice(128 * f, 128 * (f + 1))
                    products(p_H[n][:, 2 * ROWS * f + tok.start:2 * ROWS * f + tok.stop],
                             [(lambda k: w1_hi[:, k, cols], lambda k: xT_hi[:, k, used, :]),
                              (lambda k: w1_hi[:, k, cols], lambda k: xT_lo[:, k, used, :]),
                              (lambda k: w1_lo[:, k, cols], lambda k: xT_hi[:, k, used, :])], KC,
                             hid_made if f == FC - 1 else None)

            def positions(j):
                pe.wait_ge(chosen_done, j + 1)
                if j >= 1:
                    pe.wait_ge(sum_done, j)
                    pe.wait_ge(gate_done, j)
                for u in range(2):
                    to = p_P[0:ROWS, EXPERTS * u:EXPERTS * (u + 1)]
                    pe.matmul(to, ones[:, :], chosen_sum[:, :], start=True, stop=False)
                    if u == 1:
                        pe.matmul(to, ones[:, :], chosen[:, 0, :], start=False, stop=False)
                    ins = pe.matmul(to, earlier[:, :], chosen[:, u, :], start=False, stop=True)
                ins.then_inc(pos_made, 1)

            def ffn_out(i):
                u = i % 2
                pe.wait_ge(hid_done, i // 2 + 1 if i < TILES - 1 else PAIRS + 1)
                if i == 1:
                    pe.wait_ge(deg_read, 1)
                if i >= 2:
                    pe.wait_ge(out_done, i - 1)
                tok, v = slice(ROWS * u, ROWS * (u + 1)), i // 2 % 2
                products(p_Y[u][0:ROWS, :], [(lambda k: hid_hi[:, v, k, tok], lambda k: w2_hi[:, k, :]),
                                          (lambda k: hid_hi[:, v, k, tok], lambda k: w2_lo[:, k, :]),
                                          (lambda k: hid_lo[:, v, k, tok], lambda k: w2_hi[:, k, :])], FC, y_made,
                         (sf_rows[:, :], bias[:, 2, :]))

            neighbours(0)
            pe.wait_ge(counts_summed, SUMMED - 1)
            part_degrees(0, sum_of_counts[:, :])
            for b in range(SUMMED, TILES):
                pe.wait_ge(counts_in[b], 16)
                part_degrees(1 + b - SUMMED, adj[:, b, :])
            neighbours(1)
            neighbours(2)
            for j in range(PAIRS - 1):
                b, c = 2 * j, 2 * (j - 1)
                turn_xn(b)
                neighbours(b + 3)
                turn_xn(b + 1)
                if j == 0:
                    neighbours(b + 4)
                else:
                    positions(j - 1)
                    ffn_out(c)
                if b + 4 < TILES:
                    route(j)
                    if j >= 1:
                        neighbours(b + 4)
                    hidden(j)
                else:
                    hidden(j)
                    route(j)
                if 1 <= j < PAIRS - 2:
                    ffn_out(c + 1)
            ffn_out(TILES - 5)
            turn_xn(TILES - 2)
            ffn_out(TILES - 4)
            turn_xn(TILES - 1)
            ffn_out(TILES - 3)
            hidden(PAIRS - 1)
            hidden(PAIRS)
            positions(PAIRS - 2)
            route(PAIRS - 1)
            ffn_out(TILES - 2)
            ffn_out(TILES - 1)
            positions(PAIRS - 1)

        @block.vector
        def _(dve):
            steps = [0]

            def chain(ins):
                steps[0] += 1
                ins.then_inc(dve_step, 1)
                dve.wait_ge(dve_step, steps[0])

            def ts(o, i, s1, s2, op0, op1=None):
                return dve.tensor_scalar(o, i, s1, s2, op0) if op1 is None else dve.tensor_scalar(o, i, s1, s2, op0, op1)

            def stt(o, i0, s, i1, op0, op1):
                return dve.scalar_tensor_tensor(out=o, in0=i0, scalar=s, in1=i1, op0=op0, op1=op1)

            def statistics(src_ap, st, m, done):
                chain(dve.bn_stats(st, src_ap))
                dve.bn_aggr(m, st).then_inc(done, 1)

            def stats_x(t):
                dve.wait_ge(x_in[t], 16)
                if t >= 2:
                    dve.wait_ge(rstd_done, t - 1)
                    dve.wait_ge(h_done, t - 1)
                statistics(x_all[:, t, :], stats[:, t % 2, :], mv[:, t % 2, :], var_done)

            def norm_x(t):
                dve.wait_ge(var_done, t + 1)
                dve.wait_ge(rstd_done, t + 1)
                ts(h_all[:, t, :], x_all[:, t, :], mv[:, t % 2, 0:1], rstd[:, t % 2, :],
                   ALU.subtract, ALU.mult).then_inc(h_done, 1)

            def split_lo(raw, hi, lo, n):
                dve.wait_ge(w_hi_done, n + 1)
                stt(lo, raw, SW, hi, ALU.mult, ALU.subtract).then_inc(w_lo_done, 1)

            def turned_low_h(t):
                dve.wait_ge(hT_hi_done, t + 1)
                stt(hT_lo[:, t % 2, :, :].rearrange("p k n -> p (k n)"), p_T[:, 0:KC * ROWS], SH,
                    hT_hi[:, t % 2, :, :].rearrange("p k n -> p (k n)"), ALU.mult, ALU.subtract).then_inc(hT_lo_done, 1)

            dve.wait_ge(dst_in, 16)
            dve.wait_ge(const_done, 1)
            chain(dve.tensor_copy(samples[:, :], dst_all[:, ::ALIGN]))

            def compare_samples(half):
                some = slice(SAMPLES // 2 * half, SAMPLES // 2 * (half + 1))
                shape = [ROWS, GROUPS, SAMPLES // 2]
                dve.tensor_tensor(below[:, :, some], samples[:, some].unsqueeze(1).broadcast_to(shape),
                                  bounds[:, :].unsqueeze(2).broadcast_to(shape), ALU.is_lt).then_inc(below_done, 1)

            compare_samples(0)
            stats_x(0)
            compare_samples(1)
            norm_x(0)
            split_lo(wn_raw[:, 0, :], wn_hi[:, 0, :], wn_lo[:, 0, :], 0)
            dve.wait_ge(start_counted, 1)
            chain(ts(start_f[:, :], p_R[0:GROUPS, 0:1], -1.0, 0.0, ALU.add, ALU.max))
            ts(start_u[:, :], start_f[:, :], float(STARTS - 1), None, ALU.min).then_inc(start_done, 1)
            dve.wait_ge(bias_hi_done, 1)
            stt(bias_halves[:, 1, :], bias_raw[:, :], SW, bias_halves[:, 0, :], ALU.mult, ALU.subtract).then_inc(bias_done, 1)
            split_lo(wn_raw[:, 1, :], wn_hi[:, 1, :], wn_lo[:, 1, :], 1)
            turned_low_h(0)
            for k in range(2, KC):
                split_lo(wn_raw[:, k, :], wn_hi[:, k, :], wn_lo[:, k, :], k)
            stats_x(1)

            def edge_keys():
                dve.wait_ge(edges_turned, 1)
                dve.wait_ge(const_done, 6)
                s_, d_ = [p_R[:, WCHUNKS * GROUPS * kind:WCHUNKS * GROUPS * (kind + 1)].rearrange(
                    "p (c g) -> p g c", c=WCHUNKS) for kind in range(2)]
                chain(ts(tenth, s_, 1.0 / PART, 0.5 - 0.5 / PART, ALU.mult, ALU.subtract))
                stt(first_row, d_, float(PARTS), base_row[:, 0:GROUPS, :], ALU.mult, ALU.subtract)
                chain(ts(tenth, tenth, ROUND, ROUND, ALU.add, ALU.subtract))
                dve.tensor_tensor(key_col[:, 0, :, :], first_row, tenth, ALU.add).then_inc(key_cols_done, 1)
                stt(key_col[:, 1, :, :], tenth, -float(PART), s_, ALU.mult, ALU.add).then_inc(key_cols_done, 1)
                dve.wait_ge(key_cols_done, 2)
                dve.wait_ge(const_done, 7)

            def count_valid():
                ts(valid, first_row, 1.0, None, ALU.is_ge)
                d_ = p_R[:, WCHUNKS * GROUPS:2 * WCHUNKS * GROUPS].rearrange("p (c g) -> p g c", c=WCHUNKS)
                chain(stt(next_row, d_, float(PARTS), base_row[:, 1:GROUPS + 1, :], ALU.mult, ALU.subtract))
                dve.scalar_tensor_tensor(out=next_row, in0=next_row, scalar=1.0, in1=valid, op0=ALU.is_lt,
                                         op1=ALU.mult, accum_out=n_valid[:, :]).then_inc(n_valid_done, 1)

            def one_hots(duo):
                q = duo % HOT_SLOTS
                if duo >= HOT_SLOTS:
                    dve.wait_ge(counts_made, (duo - HOT_SLOTS) // 2 + 1)
                keys = key_col[:, :, 2 * duo:2 * duo + 2, :].rearrange("p k g c -> p k (g c)")
                for hot, n, first, kind in ((hot_row, HOT_ROWS, 1, 0), (hot_col, PART, 0, 1)):
                    ins = dve.tensor_tensor(hot[:, q, :, :], iota4[:, first:first + n, :],
                                            keys[:, kind:kind + 1, :].broadcast_to([128, n, 2 * WCHUNKS]), ALU.is_equal)
                ins.then_inc(hot_done, 1)

            def message_low(t):
                dve.wait_ge(g_hi_done, t + 1)
                stt(g_lo[:, t, :], p_G[0:ROWS, :], SG / (SH * SW), g_hi[:, t, :], ALU.mult, ALU.subtract).then_inc(g_lo_done, 1)

            def sum_counts(b):
                if b == 1:
                    dve.wait_ge(counts_in[0], 16)
                else:
                    dve.wait_ge(counts_summed, b - 1)
                dve.wait_ge(counts_in[b], 16)
                dve.tensor_tensor(sum_of_counts[:, :], adj[:, 0, :] if b == 1 else sum_of_counts[:, :], adj[:, b, :], ALU.add)\
                    .then_inc(counts_summed, 1)

            split_lo(ws_raw[:, 0, :], ws_hi[:, 0, :], ws_lo[:, 0, :], KC)
            norm_x(1)
            for k in range(1, KC):
                split_lo(ws_raw[:, k, :], ws_hi[:, k, :], ws_lo[:, k, :], KC + k)
            message_low(0)
            turned_low_h(1)
            stats_x(2)
            edge_keys()
            norm_x(2)
            for duo in range(4):
                one_hots(duo)
            stats_x(3)
            duo = 4
            for t in range(1, TILES):
                message_low(t)
                if t <= 2:
                    turned_low_h(t + 1)
                if t + 2 < TILES:
                    norm_x(t + 2)
                if 2 < t < TILES - 1:
                    turned_low_h(t + 1)
                if t == 1:
                    count_valid()
                if t + 1 < TILES:
                    for n in range(min(2 * BEFORE[t + 1], DUOS - duo)):
                        one_hots(duo)
                        duo += 1
                if t + 3 < TILES:
                    stats_x(t + 3)
                if t == 4:
                    split_lo(w1_raw[:], w1_hi[:], w1_lo[:], 2 * KC)
                if t == 5:
                    split_lo(wr_raw[:], wr_hi[:], wr_lo[:], 2 * KC + 1)
                if t == 3:
                    dve.wait_ge(missed_counted, 1)
                    ts(missed[:, :], p_P[0:1, 0:1], -1.0, float(N_EDGES), ALU.mult, ALU.add).then_inc(missed_done, 1)
                if t == 6:
                    split_lo(w2_raw[:], w2_hi[:], w2_lo[:], 2 * KC + 2)
                if t + 1 < TILES:
                    for _ in range(2 * AFTER[t + 1]):
                        one_hots(duo)
                        duo += 1
                if t >= TILES - 2:
                    for b in (range(1, 6) if t == TILES - 2 else range(6, SUMMED)):
                        sum_counts(b)
            assert duo == DUOS
            dve.wait_ge(missed_done, 1)

            dve.wait_ge(s_done, TILES)
            dve.wait_ge(const_done, 10)
            dve.wait_ge(xb_done, TILES)

            def general_counts():
                for t in range(TILES):
                    dve.wait_ge(counts_in[t], 16)
                dve.wait_ge(src_in, 16)
                dve.wait_ge(w_lo_done, 2 * KC + 3)
                dve.tensor_copy(all_src, src_all[:, :]).then_inc(gen_ready, 1)
                ts(all_dst, dst_all[:, :], 1.0, None, ALU.add).then_inc(gen_ready, 1)
                dve.memset(all_deg, 0.0).then_inc(gen_ready, 1)
                dve.wait_ge(gen_ready, 3)
                with dve.Fori(0, ECHUNKS) as c:
                    ts(all_src_hot, iota[0:ROWS, 0:N_NODES], all_src[:, bass.ds(c, 1)], None, ALU.is_equal)\
                        .then_inc(gen_src_hot, 1)
                    dve.wait_ge(gen_deg_made, c + 1)
                    dve.tensor_tensor(all_deg, all_deg, p_R[0:ROWS, 0:TILES], ALU.add).then_inc(gen_deg_added, 1)
                    dve.wait_ge(gen_deg_added, c + 1)
                ts(all_deg, all_deg, 1.0, SG, ALU.max, ALU.mult).then_inc(gen_ready, 1)
                dve.wait_ge(gen_ready, 4)
                dve.reciprocal(all_inv_deg, all_deg).then_inc(gen_ready, 1)
                dve.wait_ge(gen_ready, 5)
                with dve.Fori(0, TILES) as b:
                    dve.memset(all_counts, 0.0).then_inc(gen_zeroed, 1)
                    with dve.Fori(0, ECHUNKS) as c:
                        ts(all_dst_hot, iota[0:ROWS, 1:1 + ROWS], all_dst[:, bass.ds(c, 1)], None, ALU.is_equal)
                        ts(all_src_hot, iota[0:ROWS, 0:N_NODES], all_src[:, bass.ds(c, 1)], None, ALU.is_equal)\
                            .then_inc(gen_hot, 1)
                        dve.wait_ge(gen_zeroed, b + 1)
                        dve.wait_ge(gen_made, b * ECHUNKS + c + 1)
                        for (at, n), part in zip(SRC_PARTS, (p_A0, p_A1, p_S)):
                            ins = dve.tensor_tensor(all_counts[:, at:at + n], all_counts[:, at:at + n],
                                                    part[0:ROWS, 0:n], ALU.add)
                        ins.then_inc(gen_added, 1)
                        dve.wait_ge(gen_added, b * ECHUNKS + c + 1)
                    dve.tensor_copy(adj[:, bass.ds(b, 1), :], all_counts.unsqueeze(1)).then_inc(gen_adj_done, 1)
                    dve.wait_ge(gen_adj_done, b + 1)
                    dve.tensor_tensor(rest.unsqueeze(1), all_counts.unsqueeze(1), adj[:, bass.ds(b, 1), :],
                                      ALU.subtract).then_inc(gen_rest_done, 1)
                    ts(all_dst, all_dst, float(ROWS), None, ALU.subtract).then_inc(gen_moved_on, 1)
                    dve.wait_ge(gen_moved_on, b + 1)
                    for i in range(TILES):
                        dve.wait_ge(gen_fix_made, b * TILES + i + 1)
                        stt(s_all[:, i, :], p_G[0:ROWS, :], all_inv_deg[:, i:i + 1], s_all[:, i, :], ALU.mult, ALU.add)\
                            .then_inc(gen_fix_added, 1)
                        dve.wait_ge(gen_fix_added, b * TILES + i + 1)

            n_missed = dve.value_load(missed[0:1, 0:1], min_val=0, max_val=N_EDGES)
            with dve.If(n_missed > 0):
                general_counts()

            dve.wait_ge(deg_made, DEG_PARTS)
            dve.tensor_reduce(deg[:, :], p_D[0:ROWS, 0:DEG_PARTS * TILES].rearrange("p (b i) -> p i b", b=DEG_PARTS),
                              AX.X, ALU.add).then_inc(deg_read, 1)
            dve.wait_ge(deg_read, 1)
            chain(ts(deg[:, :], deg[:, :], 1.0, SG, ALU.max, ALU.mult))
            dve.reciprocal(inv_deg[:, :], deg[:, :]).then_inc(inv_deg_done, 1)
            dve.wait_ge(inv_deg_done, 1)
            with dve.If(n_missed > 0):
                dve.tensor_copy(inv_deg[:, :], all_inv_deg).then_inc(gen_ready, 1)
                dve.wait_ge(gen_ready, 6)

            def before_relu(i):
                u = i % 2
                dve.wait_ge(neigh_made, i + 1)
                stt(relu_in[:, u, :], p_N[u][0:ROWS, :], inv_deg[:, i:i + 1], s_all[:, i, :], ALU.mult, ALU.add)\
                    .then_inc(neigh_read, 1)

            def residual(i):
                u = i % 2
                dve.wait_ge(neigh_read, i + 1)
                dve.scalar_tensor_tensor(out=x1[:, u, :], in0=relu_in[:, u, :], scalar=0.0, in1=h_all[:, i, :],
                                         op0=ALU.max, op1=ALU.add, accum_out=sum1[:, u, :]).then_inc(x1_done, 1)

            def mean_1(i):
                dve.wait_ge(x1_done, i + 1)
                ts(neg_mean1[:, i % 2, :], sum1[:, i % 2, :], -1.0 / DIM, None, ALU.mult).then_inc(mean1_done, 1)

            def centre(i):
                u = i % 2
                dve.wait_ge(mean1_done, i + 1)
                stt(centred[:, u, :], x1[:, u, :], neg_mean1[:, u, :], gam[:, :], ALU.add, ALU.mult).then_inc(centred_done, 1)

            def gnn_out(i):
                u = i % 2
                dve.wait_ge(centred_done, i + 1)
                dve.wait_ge(rstd1_done, i + 1)
                dve.scalar_tensor_tensor(out=x_all[:, i, :], in0=centred[:, u, :], scalar=rstd1[:, u, :],
                                         in1=x_all[:, i, :], op0=ALU.mult, op1=ALU.add,
                                         accum_out=sum2[:, u, :]).then_inc(x2_done, 1)

            def mean_2(i):
                dve.wait_ge(x2_done, i + 1)
                ts(neg_mean2[:, i % 2, :], sum2[:, i % 2, :], -1.0 / DIM, None, ALU.mult).then_inc(mean2_done, 1)

            def norm_2(i):
                u = i % 2
                dve.wait_ge(rstd2_done, i + 1)
                if i >= 2:
                    dve.wait_ge(xT_made, i - 1)
                ts(xn[:, u, :], x_all[:, i, :], neg_mean2[:, u, :], rstd2[:, u, :], ALU.add, ALU.mult).then_inc(xn_done, 1)

            def xT_low(i):
                dve.wait_ge(xT_hi_done, i + 1)
                stt(xT_lo[:, :, i % 2, :], p_T[:, 0:KC * ROWS].rearrange("p (k n) -> p k n", k=KC), SH,
                    xT_hi[:, :, i % 2, :], ALU.mult, ALU.subtract).then_inc(xT_lo_done, 1)

            def wide(ap):
                return ap.unsqueeze(2).broadcast_to([ROWS, 2, EXPERTS])

            def best_logits(j):
                dve.wait_ge(logits_made, j + 1)
                chain(dve.tensor_reduce(top[:, :], p_R[0:ROWS, 0:2 * EXPERTS].rearrange("p (u e) -> p u e", u=2), AX.X, ALU.max))
                ts(neg_top[:, :], top[:, :], -1.0 / (SH * SW), None, ALU.mult).then_inc(top_done, 1)

            def normalise(j):
                dve.wait_ge(exp_done, j + 1)
                chain(dve.reciprocal(rsum[:, :], esum[:, :]))
                dve.tensor_tensor(probs[:, :, :], expd[:, :, :], wide(rsum[:, :]), ALU.mult).then_inc(probs_done, 1)

            def best_two(j):
                dve.wait_ge(probs_done, j + 1)
                dve.max(best[:, 0, :], probs[:, 0, :])
                chain(dve.max(best[:, 1, :], probs[:, 1, :]))
                dve.max_index(best_at[:, 0, :], best[:, 0, :], probs[:, 0, :])
                dve.max_index(best_at[:, 1, :], best[:, 1, :], probs[:, 1, :]).then_inc(best_done, 1)

            def choose(j):
                dve.wait_ge(best_done, j + 1)
                chain(dve.tensor_copy(best_f[:, :, :], best_at[:, :, :]))
                if j >= 1:
                    dve.wait_ge(sum_done, j)
                ts(first_hot[:, 0, :], iota[0:ROWS, 0:EXPERTS], best_f[:, 0, 0:1], None, ALU.is_equal)
                chain(ts(first_hot[:, 1, :], iota[0:ROWS, 0:EXPERTS], best_f[:, 1, 0:1], None, ALU.is_equal))
                for u in range(2):
                    ins = stt(chosen[:, u, :], iota[0:ROWS, 0:EXPERTS], best_f[:, u, 1:2], first_hot[:, u, :],
                              ALU.is_equal, ALU.add)
                ins.then_inc(chosen_done, 1)

            def chosen_probs(j):
                dve.wait_ge(chosen_done, j + 1)
                dve.tensor_tensor(chosen_p[:, :, :], probs[:, :, :], chosen[:, :, :], ALU.mult).then_inc(chosen_p_done, 1)

            def gates(j):
                dve.wait_ge(chosen_p_done, j + 1)
                dve.wait_ge(pos_made, j + 1)
                for u in range(2):
                    ins = dve.scalar_tensor_tensor(out=kept_p[:, u, :], in0=p_P[0:ROWS, EXPERTS * u:EXPERTS * (u + 1)],
                                                   scalar=float(CAPACITY), in1=chosen_p[:, u, :], op0=ALU.is_lt,
                                                   op1=ALU.mult, accum_out=gate[:, u, :])
                chain(ins)
                ts(gate_s[:, :, :], gate[:, :, :], 1.0 / (SF * SW), None, ALU.mult).then_inc(gate_done, 1)

            def sum_chosen(j):
                dve.wait_ge(pos_made, j + 1)
                chain(dve.tensor_tensor(chosen_sum[:, :], chosen_sum[:, :], chosen[:, 0, :], ALU.add))
                dve.tensor_tensor(chosen_sum[:, :], chosen_sum[:, :], chosen[:, 1, :], ALU.add).then_inc(sum_done, 1)

            def hidden_low(n):
                tok, j = HIDDEN_STEPS[n], min(n, PAIRS - 1)
                dve.wait_ge(hid_hi_done, n + 1)
                stt(hid_lo[:, j % 2, :, tok], hid[:, :, tok], SF, hid_hi[:, j % 2, :, tok], ALU.mult, ALU.subtract)\
                    .then_inc(hid_done, 1)

            def result(i):
                u = i % 2
                dve.wait_ge(y_made, i + 1)
                dve.wait_ge(gate_done, i // 2 + 1)
                stt(s_all[:, i, :], p_Y[u][0:ROWS, :], gate_s[:, u, :], x_all[:, i, :], ALU.mult, ALU.add).then_inc(out_done, 1)

            before_relu(0)
            residual(0)
            mean_1(0)
            centre(0)
            gnn_out(0)
            mean_2(0)
            before_relu(1)
            residual(1)
            mean_1(1)
            norm_2(0)
            centre(1)
            gnn_out(1)
            mean_2(1)
            xT_low(0)
            before_relu(2)
            residual(2)
            mean_1(2)
            norm_2(1)
            centre(2)
            for j in range(PAIRS - 2):
                b = 2 * j
                gnn_out(b + 2)
                mean_2(b + 2)
                if j >= 2:
                    result(2 * j - 3)
                norm_2(b + 2)
                before_relu(b + 3)
                if j == 0:
                    xT_low(b + 1)
                residual(b + 3)
                if j >= 1:
                    gates(j - 1)
                    sum_chosen(j - 1)
                mean_1(b + 3)
                if j >= 1:
                    result(2 * j - 2)
                centre(b + 3)
                best_logits(j)
                gnn_out(b + 3)
                normalise(j)
                mean_2(b + 3)
                best_two(j)
                choose(j)
                norm_2(b + 3)
                chosen_probs(j)
                xT_low(b + 2)
                before_relu(b + 4)
                residual(b + 4)
                hidden_low(j)
                if j < PAIRS - 3:
                    mean_1(b + 4)
                    centre(b + 4)
                    xT_low(b + 3)
            result(TILES - 7)
            before_relu(TILES - 1)
            mean_1(TILES - 2)
            xT_low(TILES - 3)
            centre(TILES - 2)
            residual(TILES - 1)
            mean_1(TILES - 1)
            gnn_out(TILES - 2)
            mean_2(TILES - 2)
            centre(TILES - 1)
            gnn_out(TILES - 1)
            mean_2(TILES - 1)
            norm_2(TILES - 2)
            gates(PAIRS - 3)
            result(TILES - 6)
            hidden_low(PAIRS - 2)
            norm_2(TILES - 1)
            xT_low(TILES - 2)
            best_logits(PAIRS - 2)
            result(TILES - 5)
            sum_chosen(PAIRS - 3)
            xT_low(TILES - 1)
            normalise(PAIRS - 2)
            best_two(PAIRS - 2)
            choose(PAIRS - 2)
            chosen_probs(PAIRS - 2)
            hidden_low(PAIRS - 1)
            gates(PAIRS - 2)
            result(TILES - 4)
            best_logits(PAIRS - 1)
            hidden_low(PAIRS)
            result(TILES - 3)
            normalise(PAIRS - 1)
            best_two(PAIRS - 1)
            sum_chosen(PAIRS - 2)
            choose(PAIRS - 1)
            chosen_probs(PAIRS - 1)
            gates(PAIRS - 1)
            result(TILES - 2)
            result(TILES - 1)


def kernel(**inputs):
    import concourse.bacc as _bacc
    from concourse.bass_utils import run_bass_kernel_spmd as _run

    src = np.ascontiguousarray(inputs["src"])
    dst = np.ascontiguousarray(inputs["dst"])
    span = WINDOW // ALIGN
    windows = np.concatenate([np.reshape(e, (N_EDGES // ALIGN, ALIGN))[k:k + STARTS]
                              for e in (src, dst) for k in range(span)], axis=1)
    arrays_in = [
        ("x", inputs["x"]), ("windows", windows), ("src", src), ("dst", dst),
        ("w_neigh_t", inputs["L0_gnn_W_neigh"].T), ("w_self_t", inputs["L0_gnn_W_self"].T),
        ("biases", np.concatenate([inputs["L0_gnn_b_neigh"], inputs["L0_gnn_b_self"], inputs["L0_ffn_b2"]])),
        ("gamma", inputs["L0_gnn_ln_gamma"]), ("beta", inputs["L0_gnn_ln_beta"]),
        ("router_t", inputs["L0_ffn_router_w"].T), ("w1_t", inputs["L0_ffn_w1"].T),
        ("b1", np.reshape(inputs["L0_ffn_b1"], (FC, 128)).T),
        ("w2_t", inputs["L0_ffn_w2"].T),
    ]
    nc = _bacc.Bacc("TRN2", target_bir_lowering=False, num_devices=1)
    arrays, args = {}, []
    for name, a in arrays_in:
        a = np.ascontiguousarray(a)
        arrays[f"in_{name}"] = a
        args.append(nc.dram_tensor(f"in_{name}", a.shape, mybir.dt.from_np(a.dtype), kind="ExternalInput").ap())
    args.append(nc.dram_tensor("counts", (GROUPS, GROUP * N_NODES), mybir.dt.float16, kind="Internal").ap())
    args.append(nc.dram_tensor("result", (N_NODES, DIM), mybir.dt.float32, kind="ExternalOutput").ap())
    gnn_ffn(nc, *args)
    r = _run(nc, [arrays], core_ids=[0])
    return r.results[0]["result"]
```
